# Optimizing a Trainium2 kernel written in Bass

```python
import numpy as np
import jax
import jax.numpy as jnp

def _softmax(x, axis=-1):
    return jax.nn.softmax(x, axis=axis)

def _gelu(x):
    return jax.nn.gelu(x, approximate=True)

def _silu(x):
    return jax.nn.silu(x)

def _sigmoid(x):
    return jax.nn.sigmoid(x)

def _layernorm(x, axis=-1, eps=1e-05):
    m = jnp.mean(x, axis=axis, keepdims=True)
    v = jnp.var(x, axis=axis, keepdims=True)
    return (x - m) / jnp.sqrt(v + eps)

def _scatter_add(tgt, idx, src, axis=0):
    return tgt.at[idx].add(src)

def _segment_sum(src, seg, n):
    return jax.ops.segment_sum(src, seg, n)
kernel_name = 'mk_seq_preln_d1_jaxref_r8_8492e7'

def setup_inputs(seed: int=0):
    np.random.seed(seed)
    _w = jnp.asarray

    def _L0_attn_setup():
        import jax, jax.numpy as jnp
        import numpy as np
        from jax import lax
        NUM_LEVELS = 2
        NUM_HEADS = 16
        LN_EPS = 1e-05
        ATTN_EPS = 1e-06

        def dwconv(x, filt):
            C = x.shape[-1]
            return lax.conv_general_dilated(x, filt[:, None, :], window_strides=(1,), padding='SAME', dimension_numbers=('NWC', 'WIO', 'NWC'), feature_group_count=C)

        def linear_attention(x, num_heads):
            B, N, C = x.shape
            d = C // num_heads
            h = x.reshape(B, N, num_heads, d)
            q = jax.nn.elu(h) + 1.0
            k = q
            v = h
            kv = jnp.einsum('bnhd,bnhe->bhde', k, v)
            z = k.sum(axis=1)
            num = jnp.einsum('bnhd,bhde->bnhe', q, kv)
            den = jnp.einsum('bnhd,bhd->bnh', q, z)[..., None] + ATTN_EPS
            return (num / den).reshape(B, N, C)

        def layer_norm(x, gamma, beta):
            mu = jnp.mean(x, axis=-1, keepdims=True)
            var = jnp.mean(jnp.square(x - mu), axis=-1, keepdims=True)
            return (x - mu) * lax.rsqrt(var + LN_EPS) * gamma + beta
        key = jax.random.key(seed)
        ks = jax.random.split(key, 7)
        B, S, C, K = (8, 512, 128, 4)
        x = jax.random.normal(ks[0], (B, S, C), dtype=jnp.float32)
        scale = 1.0 / np.sqrt(K)
        h_filter = jax.random.normal(ks[1], (K, C), dtype=jnp.float32) * scale
        g_filter = jax.random.normal(ks[2], (K, C), dtype=jnp.float32) * scale
        h_synth = jax.random.normal(ks[3], (K, C), dtype=jnp.float32) * scale
        g_synth = jax.random.normal(ks[4], (K, C), dtype=jnp.float32) * scale
        norm_gamma = jnp.ones((C,), dtype=jnp.float32)
        norm_beta = jnp.zeros((C,), dtype=jnp.float32)
        return {'x': x, 'h_filter': h_filter, 'g_filter': g_filter, 'h_synth': h_synth, 'g_synth': g_synth, 'norm_gamma': norm_gamma, 'norm_beta': norm_beta}
    _L0_attn_in = _L0_attn_setup()

    def _L0_ffn_setup():
        import jax, jax.numpy as jnp
        import numpy as np
        import math
        E = 16
        TOP_K = 2
        D = 128
        F = 512
        SH = 256
        key = jax.random.key(seed)
        ks = jax.random.split(key, 10)
        s = lambda k, shape, fan: jax.random.normal(k, shape, jnp.float32) / np.sqrt(fan)
        return {'x': jax.random.normal(ks[0], (32, 32, D), jnp.float32), 'gate_w': s(ks[1], (E, D), D), 'up_w': s(ks[2], (E, F, D), D), 'up_b': s(ks[3], (E, F), D), 'gw': s(ks[4], (E, F, D), D), 'gb': s(ks[5], (E, F), D), 'down_w': s(ks[6], (E, D, F), F), 'down_b': s(ks[7], (E, D), F), 'sh_gate_w': s(ks[8], (SH, D), D), 'sh_up_w': s(ks[9], (SH, D), D), 'sh_down_w': s(jax.random.fold_in(key, 11), (D, SH), SH)}
    _L0_ffn_in = _L0_ffn_setup()
    _d = {'L0_attn_x': _L0_attn_in['x'], 'L0_attn_h_filter': _L0_attn_in['h_filter'], 'L0_attn_g_filter': _L0_attn_in['g_filter'], 'L0_attn_h_synth': _L0_attn_in['h_synth'], 'L0_attn_g_synth': _L0_attn_in['g_synth'], 'L0_attn_norm_gamma': _L0_attn_in['norm_gamma'], 'L0_attn_norm_beta': _L0_attn_in['norm_beta'], 'L0_ffn_gate_w': _L0_ffn_in['gate_w'], 'L0_ffn_up_w': _L0_ffn_in['up_w'], 'L0_ffn_up_b': _L0_ffn_in['up_b'], 'L0_ffn_gw': _L0_ffn_in['gw'], 'L0_ffn_gb': _L0_ffn_in['gb'], 'L0_ffn_down_w': _L0_ffn_in['down_w'], 'L0_ffn_down_b': _L0_ffn_in['down_b'], 'L0_ffn_sh_gate_w': _L0_ffn_in['sh_gate_w'], 'L0_ffn_sh_up_w': _L0_ffn_in['sh_up_w'], 'L0_ffn_sh_down_w': _L0_ffn_in['sh_down_w']}
    _x0 = _d['L0_attn_x']
    _d['L0_attn_x'] = jax.random.normal(jax.random.fold_in(jax.random.key(seed), 1), (2, 1024, 128), dtype=_x0.dtype)
    del _x0
    return _d

def reference(L0_attn_x, L0_attn_h_filter, L0_attn_g_filter, L0_attn_h_synth, L0_attn_g_synth, L0_attn_norm_gamma, L0_attn_norm_beta, L0_ffn_gate_w, L0_ffn_up_w, L0_ffn_up_b, L0_ffn_gw, L0_ffn_gb, L0_ffn_down_w, L0_ffn_down_b, L0_ffn_sh_gate_w, L0_ffn_sh_up_w, L0_ffn_sh_down_w):

    def _L0_attn_ref(x, h_filter, g_filter, h_synth, g_synth, norm_gamma, norm_beta):
        import jax, jax.numpy as jnp
        import numpy as np
        from jax import lax
        NUM_LEVELS = 2
        NUM_HEADS = 16
        LN_EPS = 1e-05
        ATTN_EPS = 1e-06

        def dwconv(x, filt):
            C = x.shape[-1]
            return lax.conv_general_dilated(x, filt[:, None, :], window_strides=(1,), padding='SAME', dimension_numbers=('NWC', 'WIO', 'NWC'), feature_group_count=C)

        def linear_attention(x, num_heads):
            B, N, C = x.shape
            d = C // num_heads
            h = x.reshape(B, N, num_heads, d)
            q = jax.nn.elu(h) + 1.0
            k = q
            v = h
            kv = jnp.einsum('bnhd,bnhe->bhde', k, v)
            z = k.sum(axis=1)
            num = jnp.einsum('bnhd,bhde->bnhe', q, kv)
            den = jnp.einsum('bnhd,bhd->bnh', q, z)[..., None] + ATTN_EPS
            return (num / den).reshape(B, N, C)

        def layer_norm(x, gamma, beta):
            mu = jnp.mean(x, axis=-1, keepdims=True)
            var = jnp.mean(jnp.square(x - mu), axis=-1, keepdims=True)
            return (x - mu) * lax.rsqrt(var + LN_EPS) * gamma + beta
        low = x
        highs = []
        lens = []
        for _ in range(NUM_LEVELS):
            lens.append(low.shape[1])
            l = dwconv(low, h_filter)[:, ::2]
            h = dwconv(low, g_filter)[:, ::2]
            highs.append(h)
            low = l
        low = linear_attention(low, NUM_HEADS)
        for h, L in zip(reversed(highs), reversed(lens)):
            up_l = jnp.repeat(low, 2, axis=1)[:, :L]
            up_h = jnp.repeat(h, 2, axis=1)[:, :L]
            low = dwconv(up_l, h_synth) + dwconv(up_h, g_synth)
        return layer_norm(x + low, norm_gamma, norm_beta)

    def _L0_ffn_ref(x, gate_w, up_w, up_b, gw, gb, down_w, down_b, sh_gate_w, sh_up_w, sh_down_w):
        import jax, jax.numpy as jnp
        import numpy as np
        import math
        E = 16
        TOP_K = 2
        D = 128
        F = 512
        SH = 256
        B, S, Dm = x.shape
        h = x.reshape(-1, Dm)
        T = h.shape[0]
        scores = jax.nn.sigmoid(h @ gate_w.T)
        cap = math.ceil(T / E * TOP_K)
        topk_score, topk_ids = jax.lax.top_k(scores.T, cap)
        xin = h[topk_ids]
        up = jnp.einsum('ecd,efd->ecf', xin, up_w) + up_b[:, None, :]
        g = jnp.einsum('ecd,efd->ecf', xin, gw) + gb[:, None, :]
        eo = jax.nn.silu(g) * up
        eo = jnp.einsum('ecf,edf->ecd', eo, down_w) + down_b[:, None, :]
        flat = (eo * topk_score[..., None]).reshape(-1, Dm)
        out = jnp.zeros_like(h).at[topk_ids.reshape(-1)].add(flat)
        out = out.reshape(B, S, Dm)
        shared = jax.nn.silu(jnp.einsum('bsd,fd->bsf', x, sh_gate_w)) * jnp.einsum('bsd,fd->bsf', x, sh_up_w)
        shared = jnp.einsum('bsf,df->bsd', shared, sh_down_w)
        return out + shared
    x = L0_attn_x
    x = x + _L0_attn_ref(_layernorm(x, axis=-1), L0_attn_h_filter, L0_attn_g_filter, L0_attn_h_synth, L0_attn_g_synth, L0_attn_norm_gamma, L0_attn_norm_beta)
    x = x + _L0_ffn_ref(_layernorm(x, axis=-1), L0_ffn_gate_w, L0_ffn_up_w, L0_ffn_up_b, L0_ffn_gw, L0_ffn_gb, L0_ffn_down_w, L0_ffn_down_b, L0_ffn_sh_gate_w, L0_ffn_sh_up_w, L0_ffn_sh_down_w)
    return x

_drawn_inputs = setup_inputs


def setup_inputs(seed=0):
    import zlib

    import numpy as np

    out = dict(_drawn_inputs(seed))
    spreads = {'L0_attn_norm_gamma': (1.0, 0.2), 'L0_attn_norm_beta': (0.0, 0.1)}
    factors = {}
    for name, (base, spread) in spreads.items():
        noise = np.random.default_rng([zlib.crc32(name.encode()), seed]).standard_normal(out[name].shape)
        drawn = base * np.exp(spread * noise) if base else spread * noise
        out[name] = jnp.asarray(drawn.astype(out[name].dtype))
    for name, factor in factors.items():
        out[name] = (out[name] * factor).astype(out[name].dtype)
    return out
```

```python
from contextlib import ExitStack

import concourse.bass as bass
from concourse import mybir

ALU = mybir.AluOpType
ACT = mybir.ActivationFunctionType
AX = mybir.AxisListType
F32 = mybir.dt.float32
F16 = mybir.dt.float16
BF16 = mybir.dt.bfloat16
I32 = mybir.dt.int32
U32 = mybir.dt.uint32

P = 128
LN_EPS = 1e-5
ATTN_EPS = 1e-6
HEAD = 8


def wavelet_attention_moe(nc, x, h_filter, g_filter, h_synth, g_synth, gamma, beta, gate_w, up_w, up_b,
                          gw, gb, down_w, down_b, sh_gate_w, sh_up_w, sh_down_w, out):
    NB, SEQ, C = x.shape
    TOK = NB * SEQ
    E, F, _ = up_w.shape
    FT = F // P
    SHT = sh_gate_w.shape[0] // P
    CAP = -(-TOK * 2 // E)
    BLK = TOK // 256
    BPB = BLK // NB
    NT = TOK // P
    N1, N2 = SEQ // 2, SEQ // 4
    ROW = C + E
    KINDS = 3
    GROUPS = E * KINDS
    RING = 8
    CH = CAP // P
    BITS = 30
    HI = 16

    h_rows = nc.dram_tensor("h_rows", [TOK, ROW], F32)

    ctx = ExitStack()
    with ctx:
        ctx.enter_context(nc.allow_low_precision(reason="exact integers"))

        def sb(name, shape, dt=F32):
            return ctx.enter_context(nc.sbuf_tensor(name, shape, dt))

        def sem(name):
            return ctx.enter_context(nc.semaphore(name))

        bank = [ctx.enter_context(nc.psum_tensor(f"bank{i}", [P, 512], F32)) for i in range(8)]

        ident = sb("ident", [P, P])
        same8 = sb("same8", [P, P])
        same8_bf = sb("same8_bf", [P, P], BF16)
        earlier = sb("earlier", [P, P], BF16)
        pick = sb("pick", [P, 8])
        sel_lo = sb("sel_lo", [HI, P])
        token_no = sb("token_no", [P, 2 * P], F16)
        half_pow = sb("half_pow", [P, NT])
        filt_rows = sb("filt_rows", [16, C])
        gate_rows = sb("gate_rows", [E, C])
        bias_rows = sb("bias_rows", [E, 2, F])
        gamma_bc = sb("gamma_bc", [P, C])
        beta_bc = sb("beta_bc", [P, C])
        consts = sb("consts", [P, 160])
        taps = consts[:, 0:16]
        gate_wT = consts[:, 16:32]
        biasT = consts[:, 32:160].rearrange("p (k j e) -> p k j e", k=2, j=FT)
        comb = sb("comb", [P, 2, 3])
        diag = sb("diag", [P, 14, P])
        sh_wT = sb("sh_wT", [P, 6, P])

        x_tok = sb("x_tok", [P, NT, C])
        x1 = sb("x1", [P, NT, C])
        hrow = sb("hrow", [P, NT, ROW])
        hT = sb("hT", [P, NT, P])
        wT = sb("wT", [P, E, KINDS, FT, P])
        raw = sb("raw", [P, RING, F])

        area = sb("area", [P, 2048 + 4 * 514 + 2 * 516 + 2 * 514 * 2 + 4 * 258])
        at = [0]

        def carve(n, base=None):
            if base is not None:
                at[0] = base
            a = area[:, at[0]:at[0] + n]
            at[0] += n
            return a

        xn_tok = carve(2048, 0).rearrange("p (i c) -> p i c", i=NT)
        xp = carve(4 * 514).rearrange("p (r b n) -> p r b n", r=2, b=NB)
        l1p = carve(2 * 516).rearrange("p (b n) -> p b n", b=NB)
        h1p = carve(2 * 514).rearrange("p (b n) -> p b n", b=NB)
        r1p = carve(2 * 514).rearrange("p (b n) -> p b n", b=NB)
        h2p = carve(2 * 258).rearrange("p (b n) -> p b n", b=NB)
        ap_ = carve(2 * 258).rearrange("p (b n) -> p b n", b=NB)
        one_hi = carve(2048, 0).bitcast(F16).rearrange("p (n a e) -> p n a e", a=HI, e=8)
        one_lo = carve(2048).bitcast(F16).rearrange("p (n b e) -> p n b e", b=HI, e=8)
        sel = carve(5 * 256).rearrange("p (k n) -> p k n", k=5)
        sh_hid = carve(2 * 512).rearrange("p (t n) -> p t n", t=2)
        slot_i = carve(3 * 256).bitcast(I32).rearrange("p (k n) -> p k n", k=3)
        slot_h = carve(256).bitcast(F16).rearrange("p (k n) -> p k n", k=2)
        ext = carve(256)
        score2 = carve(256)
        gath = carve(3 * CH * ROW, 4104).rearrange("p (s c r) -> p s c r", s=3, c=CH)
        xselT = carve(2 * CAP).rearrange("p (s n) -> p s n", s=2)
        hidden = carve(2 * FT * CAP).rearrange("p (s j n) -> p s j n", s=2, j=FT)
        eo = carve(2 * CH * C).rearrange("p (s c d) -> p s c d", s=2, c=CH)
        flat_hT = hT[:, :, :].rearrange("p i t -> p (i t)")
        flat_hrow = hrow[:, :, :].rearrange("p i t -> p (i t)")
        l2f, expf, qf, vT = (flat_hT[:, 512 * k:512 * k + 512] for k in range(4))
        kT, den = (flat_hrow[:, 512 * k:512 * k + 512] for k in range(2))
        sh_raw = x1[:, 0:6, :]
        kvz = x1[:, 8:12, :].rearrange("p (z b) c -> p z b c", z=2)
        down_b_bc = x_tok
        junk = sb("junk", [P, 256], BF16)
        sgate = sb("sgate", [P, 2, 512])
        stats = sb("stats", [P, NT, 6])
        small = sb("small", [P, 8, NT])
        zsum = sb("zsum", [P, 2])
        cnt = sb("cnt", [P, 4], BF16)
        ibits = sb("ibits", [P, 4], I32)
        rneed = sb("rneed", [P, 1])
        itab = sb("itab", [P, 32])
        itabT = sb("itabT", [HI, 256])
        rows = sb("rows", [P, 2, CH, 8], U32)

        s_x = [sem(f"s_x{b}") for b in range(NB)]
        s_small_in = sem("s_small_in")
        s_gamma = sem("s_gamma")
        s_sh_in = sem("s_sh_in")
        s_db_in = sem("s_db_in")
        s_raw = [sem(f"s_raw{i}") for i in range(RING)]
        s_ident = sem("s_ident")
        s_pool = sem("s_pool")
        s_masks = sem("s_masks")
        s_diag = sem("s_diag")
        s_comb = sem("s_comb")
        s_xb = sem("s_xb")
        s_var = sem("s_var")
        s_rstd = sem("s_rstd")
        s_constT = sem("s_constT")
        s_const = sem("s_const")
        s_shT = sem("s_shT")
        s_shw = sem("s_shw")
        s_wTp = sem("s_wTp")
        s_wT = sem("s_wT")
        s_pad = sem("s_pad")
        s_xn = sem("s_xn")
        s_xnT = sem("s_xnT")
        s_xp = sem("s_xp")
        s_l1 = sem("s_l1")
        s_l2 = sem("s_l2")
        s_h1 = sem("s_h1")
        s_h1e = sem("s_h1e")
        s_h2 = sem("s_h2")
        s_h2e = sem("s_h2e")
        s_exp = sem("s_exp")
        s_q = sem("s_q")
        s_qvT = sem("s_qvT")
        s_qve = sem("s_qve")
        s_kv = sem("s_kv")
        s_kvm = sem("s_kvm")
        s_nd = sem("s_nd")
        s_attn = sem("s_attn")
        s_up2 = sem("s_up2")
        s_r1 = sem("s_r1")
        s_up1 = sem("s_up1")
        s_t = sem("s_t")
        s_hn = sem("s_hn")
        s_hTp = sem("s_hTp")
        s_hT = sem("s_hT")
        s_logit = sem("s_logit")
        s_score = sem("s_score")
        s_scT = sem("s_scT")
        s_hrow = sem("s_hrow")
        s_hstore = sem("s_hstore")
        s_cnt = sem("s_cnt")
        s_tot = sem("s_tot")
        s_shgu = sem("s_shgu")
        s_shsil = sem("s_shsil")
        s_shhid = sem("s_shhid")
        s_shout = sem("s_shout")
        s_base = sem("s_base")
        s_store = sem("s_store")
        s_need = sem("s_need")
        s_pos = sem("s_pos")
        s_posT = sem("s_posT")
        s_hot = sem("s_hot")
        s_tab = sem("s_tab")
        s_itab = sem("s_itab")
        s_itT = sem("s_itT")
        s_itTe = sem("s_itTe")
        s_spread = sem("s_spread")
        s_rows = sem("s_rows")
        s_gath = [sem(f"s_gath{i}") for i in range(3)]
        s_xsT = sem("s_xsT")
        s_xs = sem("s_xs")
        s_gu = sem("s_gu")
        s_sil = sem("s_sil")
        s_hid = sem("s_hid")
        s_dn = sem("s_dn")
        s_eb = sem("s_eb")
        s_eo = sem("s_eo")
        s_scat = sem("s_scat")
        s_dve = sem("s_dve")
        s_act = sem("s_act")

        x_v = x.rearrange("b (k p r) c -> p (b k) (r c)", p=P, r=2)
        out_v = out.rearrange("b (k p r) c -> p (b k) (r c)", p=P, r=2)
        out_rows = out.rearrange("b s c -> (b s) c")
        h_v = h_rows[:, :].rearrange("(k p r) c -> p k (r c)", p=P, r=2)
        up_v = up_w.rearrange("e (p j) d -> e p (j d)", j=FT)
        gw_v = gw.rearrange("e (p j) d -> e p (j d)", j=FT)

        def tiles(b):
            return slice(b * NT // NB, (b + 1) * NT // NB)

        FILL = dict(start=6, lift=4, band=4, attn=4, up=4, norm=4, shared=12)
        FILL["search"] = GROUPS - sum(FILL.values())
        TURNS = {24 + k: 2 for k in range(1, 6)}
        TURNS.update({6 * n + 5: 2 for n in range(4)})
        TURNS.update({6 * n + 6: 1 for n in range(4)})
        assert FILL["search"] == 10

        block = ctx.enter_context(nc.Block())

        @block.sync
        def _(sp):
            for b in range(NB):
                sp.dma_start(x_tok[:, tiles(b), :].rearrange("p (k r) c -> p k (r c)", r=2),
                             x_v[:, b * BPB:(b + 1) * BPB, :]).then_inc(s_x[b], 16)
            for k in range(GROUPS):
                e, kind = divmod(k, KINDS)
                if k >= RING:
                    sp.wait_ge(s_wTp, k - RING + 1)
                src = (up_v, gw_v, down_w)[kind][e]
                sp.dma_start(raw[:, k % RING, :], src).then_inc(s_raw[k % RING], 16)
            for b in range(NB):
                sp.wait_ge(s_hn, 2 * (b + 1))
                sp.wait_ge(s_hrow, 1)
                sp.dma_start(h_v[:, b * BPB:(b + 1) * BPB, :],
                             hrow[:, tiles(b), :].rearrange("p (k r) c -> p k (r c)", r=2)).then_inc(s_hstore, 16)
            sp.dma_start(down_b_bc[:, :, :].rearrange("p e c -> p (e c)"),
                         down_b.rearrange("e c -> (e c)").partition_broadcast(P)).then_inc(s_db_in, 16)
            for n in range(NT // 4):
                sp.wait_ge(s_base, n + 1)
                sp.dma_start(out_v[:, 2 * n:2 * n + 2, :],
                             x1[:, 4 * n:4 * n + 4, :].rearrange("p (k r) c -> p k (r c)", r=2)).then_inc(s_store, 16)
            sp.wait_ge(s_hstore, 16 * NB)
            sp.wait_ge(s_store, 16 * (NT // 4))
            sp.wait_ge(s_scat, 16 * CH * E)

        @block.gpsimd
        def _(pool):
            step = [0]

            def link(ins):
                step[0] += 1
                ins.then_inc(s_pool, 1)
                pool.wait_ge(s_pool, step[0])

            link(pool.memset(ident[:, :], 0.0))
            pool.affine_select(out=ident[:, :], in_=ident[:, :], compare_op=ALU.not_equal, fill=1.0, base=0,
                               pattern=[[-1, P]], channel_multiplier=1).then_inc(s_ident, 1)
            pool.memset(half_pow[:, :], -0.5)
            pool.memset(xp[:, :, :, 0:1], 0.0)
            pool.memset(xp[:, :, :, N1 + 1:N1 + 2], 0.0)
            pool.memset(l1p[:, :, 0:1], 0.0)
            pool.memset(l1p[:, :, N1 + 1:N1 + 4], 0.0)
            for band, n in ((h1p, N1), (r1p, N1), (h2p, N2), (ap_, N2)):
                pool.memset(band[:, :, 0:1], 0.0)
                last = pool.memset(band[:, :, n + 1:n + 2], 0.0)
            last.then_inc(s_pad, 1)
            link(pool.memset(same8[:, :], 1.0))
            link(pool.affine_select(out=same8[:, :], in_=same8[:, :], compare_op=ALU.is_ge, fill=0.0, base=0,
                                    pattern=[[-8, 16], [0, 8]], channel_multiplier=1))
            link(pool.affine_select(out=same8[:, :], in_=same8[:, :], compare_op=ALU.is_ge, fill=0.0, base=7,
                                    pattern=[[8, 16], [0, 8]], channel_multiplier=-1))
            pool.tensor_copy(same8_bf[:, :], same8[:, :])
            pool.affine_select(out=earlier[:, :], in_=same8[:, :], compare_op=ALU.is_ge, fill=0.0, base=-1,
                               pattern=[[1, P]], channel_multiplier=-1)
            link(pool.memset(sel_lo[:, :], 1.0))
            link(pool.affine_select(out=sel_lo[:, :], in_=sel_lo[:, :], compare_op=ALU.is_ge, fill=0.0, base=0,
                                    pattern=[[1, P]], channel_multiplier=-8))
            link(pool.affine_select(out=sel_lo[:, :], in_=sel_lo[:, :], compare_op=ALU.is_ge, fill=0.0, base=7,
                                    pattern=[[-1, P]], channel_multiplier=8))
            pool.iota(token_no[:, :], pattern=[[1, 2], [256, BLK], [0, E]], base=0, channel_multiplier=2,
                      allow_small_or_imprecise_dtypes=True).then_inc(s_masks, 1)

            def rsqrt(n, w):
                pool.wait_ge(s_var, n + 1)
                v = small[:, 5, w]
                link(pool.tensor_scalar(v, v, LN_EPS, None, ALU.add))
                pool.tensor_tensor(small[:, 6, w], v, half_pow[:, w], ALU.pow).then_inc(s_rstd, 1)

            rsqrt(0, tiles(0))
            rsqrt(1, tiles(1))
            pool.wait_ge(s_const, 1)
            for k in range(4):
                pool.tensor_scalar(diag[:, k, :], ident[:, :], taps[:, 4 + k:5 + k], None, ALU.mult)
            pool.wait_ge(s_comb, 1)
            for f in range(2):
                tap = [taps[:, 8 + 4 * f:9 + 4 * f], comb[:, f, 2:3], taps[:, 11 + 4 * f:12 + 4 * f],
                       comb[:, f, 0:1], comb[:, f, 1:2]]
                for k in range(5):
                    last = pool.tensor_scalar(diag[:, 4 + 5 * f + k, :], ident[:, :], tap[k], None, ALU.mult)
            last.then_inc(s_diag, 1)
            pool.wait_ge(s_gamma, 32)
            pool.wait_ge(s_xn, 2 * NB)
            pool.tensor_tensor(x_tok[:, :, :], x_tok[:, :, :],
                               beta_bc[:, :].unsqueeze(1).to_broadcast([P, NT, C]), ALU.add).then_inc(s_xb, 1)
            for n in range(2, 6):
                rsqrt(n, tiles(n % 2))

            def gather(e):
                g, k = divmod(e, 8)
                if e >= 3:
                    pool.wait_ge(s_eo, CH * (e - 2))
                for c in range(CH):
                    pool.indirect_dma_start(out=gath[:, e % 3, c, :], out_offset=None, in_=h_rows[:, :],
                                            in_offset=bass.IndirectOffsetOnAxis(ap=rows[:, g, c, k:k + 1], axis=0),
                                            ).then_inc(s_gath[e % 3], 16)

            def scatter(e):
                g, k = divmod(e, 8)
                pool.wait_ge(s_eo, CH * (e + 1))
                if e == 0:
                    pool.wait_ge(s_store, 16 * (NT // 4))
                else:
                    pool.wait_ge(s_scat, 16 * CH * e)
                for c in range(CH):
                    pool.indirect_dma_start(out=out_rows, in_=eo[:, e % 2, c, :], in_offset=None,
                                            out_offset=bass.IndirectOffsetOnAxis(ap=rows[:, g, c, k:k + 1], axis=0),
                                            compute_op=ALU.add).then_inc(s_scat, 16)

            pool.wait_ge(s_rows, 1)
            pool.wait_ge(s_hstore, 16 * NB)
            gather(0)
            gather(1)
            gather(2)
            for e in range(E):
                scatter(e)
                if e + 3 < E:
                    gather(e + 3)

        def weigh(act, e):
            act.wait_ge(s_eb, e + 1)
            for c in range(CH):
                act.activation(eo[:, e % 2, c, :], eo[:, e % 2, c, :], ACT.Copy,
                               scale=gath[:, e % 3, c, C + e:C + e + 1]).then_inc(s_eo, 1)

        @block.scalar
        def _(act):
            for r, src in enumerate((h_filter, g_filter, h_synth, g_synth)):
                act.dma_start(filt_rows[4 * r:4 * r + 4, :], src).then_inc(s_small_in, 16)
            act.dma_start(gate_rows[:, :], gate_w).then_inc(s_small_in, 16)
            act.dma_start(bias_rows[:, 0, :], up_b).then_inc(s_small_in, 16)
            act.dma_start(bias_rows[:, 1, :], gb).then_inc(s_small_in, 16)
            act.dma_start(gamma_bc[:, :], gamma.partition_broadcast(P)).then_inc(s_gamma, 16)
            act.dma_start(beta_bc[:, :], beta.partition_broadcast(P)).then_inc(s_gamma, 16)
            act.dma_start(sh_raw[:, 0:2, :], sh_gate_w.rearrange("(t p) d -> p t d", p=P)).then_inc(s_sh_in, 16)
            act.dma_start(sh_raw[:, 2:4, :], sh_up_w.rearrange("(t p) d -> p t d", p=P)).then_inc(s_sh_in, 16)
            act.dma_start(sh_raw[:, 4:6, :].rearrange("p t d -> p (t d)"), sh_down_w).then_inc(s_sh_in, 16)

            done_w = [0]

            def keep_weights(n):
                for _ in range(n):
                    k = done_w[0]
                    done_w[0] += 1
                    act.wait_ge(s_wTp, k + 1)
                    e, kind = divmod(k, KINDS)
                    act.copy(wT[:, e, kind, :, :].rearrange("p j f -> p (j f)"), bank[6 + k % 2][:, :]).then_inc(s_wT, 1)

            act.wait_ge(s_constT, 1)
            act.copy(consts[:, :], bank[5][:, 0:160]).then_inc(s_const, 1)
            keep_weights(FILL["start"])
            act.wait_ge(s_pad, 1)
            for b in range(NB):
                for r in range(2):
                    act.wait_ge(s_xnT, 2 * b + r + 1)
                    act.copy(xp[:, r, b, 1:N1 + 1], bank[2 * b + r][:, :]).then_inc(s_xp, 1)
            keep_weights(FILL["lift"])
            for b in range(NB):
                act.wait_ge(s_h1, b + 1)
                act.copy(h1p[:, b, 1:N1 + 1], bank[b][:, :]).then_inc(s_h1e, 1)
            act.wait_ge(s_shT, 1)
            act.copy(sh_wT[:, 0:4, :].rearrange("p t f -> p (t f)"), bank[4][:, :])
            act.copy(sh_wT[:, 4:6, :].rearrange("p t f -> p (t f)"), bank[5][:, 256:512]).then_inc(s_shw, 1)
            keep_weights(FILL["band"])
            act.wait_ge(s_h2, 1)
            act.copy(h2p[:, :, 1:N2 + 1], bank[0][:, :].rearrange("p (b n) -> p b n", b=NB)).then_inc(s_h2e, 1)
            act.wait_ge(s_l2, 1)
            act.activation(expf[:, :], l2f[:, :], ACT.Exp).then_inc(s_exp, 1)
            act.wait_ge(s_qvT, 1)
            act.copy(vT[:, :], bank[1][:, :]).then_inc(s_qve, 1)
            keep_weights(FILL["attn"])
            act.wait_ge(s_up2, 1)
            act.copy(r1p[:, :, 2:N1 + 2:2], bank[5][:, :].rearrange("p (b n) -> p b n", b=NB)).then_inc(s_r1, 1)
            keep_weights(FILL["up"])
            keep_weights(FILL["norm"])
            for n in range(4):
                act.wait_ge(s_hTp, n + 1)
                act.copy(hT[:, 4 * n:4 * n + 4, :].rearrange("p i t -> p (i t)"), bank[n][:, :]).then_inc(s_hT, 1)
            act.wait_ge(s_logit, 1)
            act.activation(sel[:, 0, :], bank[4][:, 0:256], ACT.Sigmoid).then_inc(s_score, 1)
            act.wait_ge(s_score, 1)
            act.copy(hrow[:, :, C:ROW].rearrange("p (k r) e -> p k r e", r=2),
                     sel[:, 0, :].rearrange("p (r e k) -> p k r e", r=2, e=E)).then_inc(s_hrow, 1)
            per = FILL["shared"] // 4
            for n in range(4):
                act.wait_ge(s_shgu, n + 1)
                if n:
                    act.wait_ge(s_shhid, n)
                for t in range(SHT):
                    last = act.activation(sgate[:, t, :], bank[t][:, :], ACT.Silu)
                last.then_inc(s_shsil, 1)
                keep_weights(per)
            keep_weights(FILL["search"])
            for q in range(E * FT):
                e, j = divmod(q, FT)
                act.wait_ge(s_gu, q + 1)
                if q >= 2:
                    act.wait_ge(s_hid, q - 1)
                act.activation(sgate[:, q % 2, 0:CAP], bank[q % 3][:, CAP:2 * CAP], ACT.Silu,
                               bias=biasT[:, 1, j, e:e + 1]).then_inc(s_sil, 1)
                if j == 2 and e > 0:
                    weigh(act, e - 1)
            weigh(act, E - 1)

        @block.vector
        def _(dve):
            step = [0]

            def link(ins):
                step[0] += 1
                ins.then_inc(s_dve, 1)
                dve.wait_ge(s_dve, step[0])

            def norm_stats(src, w):
                for i in range(w.start, w.stop):
                    last = dve.bn_stats(stats[:, i, :], src[:, i, 0:C])
                link(last)
                m_e, v_e, m_o, v_o = (stats[:, w, k] for k in (1, 2, 4, 5))
                dve.tensor_tensor(small[:, 1, w], m_e, m_o, ALU.subtract)
                dve.tensor_tensor(small[:, 2, w], v_e, v_o, ALU.add)
                link(dve.tensor_tensor(small[:, 0, w], m_e, m_o, ALU.add))
                link(dve.scalar_tensor_tensor(small[:, 3, w], small[:, 1, w], 0.25, small[:, 1, w], ALU.mult, ALU.mult))
                dve.scalar_tensor_tensor(small[:, 5, w], small[:, 2, w], 1.0 / C, small[:, 3, w],
                                         ALU.mult, ALU.add).then_inc(s_var, 1)

            def norm_apply(dst, src, w, sem_done, n):
                dve.wait_ge(s_rstd, n)
                link(dve.scalar_tensor_tensor(small[:, 4, w], small[:, 0, w], -0.5, small[:, 6, w], ALU.mult, ALU.mult))
                for i in range(w.start, w.stop):
                    last = dve.tensor_scalar(dst[:, i, 0:C], src[:, i, :], small[:, 6, i:i + 1], small[:, 4, i:i + 1],
                                             ALU.mult, ALU.add)
                    if i % 4 == 3:
                        last.then_inc(sem_done, 1)

            dve.wait_ge(s_ident, 1)
            dve.tensor_reduce(pick[:, :], ident[:, :].rearrange("p (a e) -> p e a", e=8), AX.X, ALU.add)
            for b in range(NB):
                dve.wait_ge(s_x[b], 16)
                norm_stats(x_tok, tiles(b))
            for b in range(NB):
                norm_apply(xn_tok, x_tok, tiles(b), s_xn, b + 1)
            dve.wait_ge(s_const, 1)
            syn = taps[:, 8:16].rearrange("p (f k) -> p f k", f=2)
            dve.tensor_tensor(comb[:, :, 0:1], syn[:, :, 0:1], syn[:, :, 1:2], ALU.add)
            dve.tensor_tensor(comb[:, :, 1:2], syn[:, :, 2:3], syn[:, :, 3:4], ALU.add)
            dve.tensor_tensor(comb[:, :, 2:3], syn[:, :, 1:2], syn[:, :, 2:3], ALU.add).then_inc(s_comb, 1)
            for b in range(NB):
                dve.wait_ge(s_xp, 2 * b + 2)
                dst = l1p[:, b, 1:N1 + 1]
                link(dve.tensor_scalar(dst, xp[:, 1, b, 0:N1], taps[:, 0:1], None, ALU.mult))
                for k, (r, o) in ((1, (0, 1)), (2, (1, 1)), (3, (0, 2))):
                    ins = dve.scalar_tensor_tensor(dst, xp[:, r, b, o:o + N1], taps[:, k:k + 1], dst, ALU.mult, ALU.add)
                    if k < 3:
                        link(ins)
                ins.then_inc(s_l1, 1)
            dve.wait_ge(s_l1, NB)
            l2 = l2f[:, :].rearrange("p (b n) -> p b n", b=NB)
            link(dve.tensor_scalar(l2, l1p[:, :, 0:N1:2], taps[:, 0:1], None, ALU.mult))
            for k in range(1, 4):
                ins = dve.scalar_tensor_tensor(l2, l1p[:, :, k:k + N1:2], taps[:, k:k + 1], l2, ALU.mult, ALU.add)
                if k < 3:
                    link(ins)
            ins.then_inc(s_l2, 1)
            dve.wait_ge(s_l2, 1)
            link(dve.tensor_scalar(qf[:, :], l2f[:, :], 0.0, None, ALU.max))
            dve.wait_ge(s_exp, 1)
            dve.scalar_tensor_tensor(qf[:, :], expf[:, :], 1.0, qf[:, :], ALU.min, ALU.add).then_inc(s_q, 1)
            dve.wait_ge(s_q, 1)
            link(dve.tensor_reduce(zsum[:, :], qf[:, :].rearrange("p (b n) -> p b n", b=NB), AX.X, ALU.add))
            dve.wait_ge(s_qvT, 2)
            dve.tensor_copy(kT[:, :], bank[2][:, :]).then_inc(s_qve, 1)
            dve.wait_ge(s_masks, 1)
            for b in range(NB):
                dve.tensor_scalar(kvz[:, 1, b, :], same8[:, :], zsum[:, b:b + 1], None, ALU.mult)
            dve.wait_ge(s_kv, 1)
            dve.tensor_tensor(kvz[:, 0, :, :], bank[3][:, 0:256].rearrange("p (b n) -> p b n", b=NB),
                              same8[:, :].unsqueeze(1).to_broadcast([P, NB, P]), ALU.mult).then_inc(s_kvm, 1)
            dve.wait_ge(s_nd, 1)
            link(dve.tensor_scalar(den[:, :], bank[1][:, :], ATTN_EPS, None, ALU.add))
            link(dve.reciprocal(den[:, :], den[:, :]))
            dve.tensor_tensor(ap_[:, :, 1:N2 + 1], bank[2][:, :].rearrange("p (b n) -> p b n", b=NB),
                              den[:, :].rearrange("p (b n) -> p b n", b=NB), ALU.mult).then_inc(s_attn, 1)
            dve.wait_ge(s_up2, 1)
            dve.tensor_copy(r1p[:, :, 1:N1 + 1:2], bank[4][:, :].rearrange("p (b n) -> p b n", b=NB)).then_inc(s_r1, 1)
            for n in range(4):
                dve.wait_ge(s_up1, n + 1)
                link(dve.tensor_tensor(x1[:, 4 * n:4 * n + 4, :].rearrange("p i c -> p (i c)"), bank[n][:, :],
                                       xn_tok[:, 4 * n:4 * n + 4, :].rearrange("p i c -> p (i c)"), ALU.add))
            dve.wait_ge(s_gamma, 32)
            dve.wait_ge(s_xb, 1)
            for b in range(NB):
                norm_stats(x1, tiles(b))
            for b in range(NB):
                w = tiles(b)
                dve.wait_ge(s_rstd, 3 + b)
                link(dve.tensor_scalar(small[:, 4, w], small[:, 0, w], 0.5, None, ALU.mult))
                for i in range(w.start, w.stop):
                    last = dve.scalar_tensor_tensor(x1[:, i, :], x1[:, i, :], small[:, 4, i:i + 1], gamma_bc[:, :],
                                                    ALU.subtract, ALU.mult)
                link(last)
                for i in range(w.start, w.stop):
                    last = dve.scalar_tensor_tensor(x1[:, i, :], x1[:, i, :], small[:, 6, i:i + 1], x_tok[:, i, :],
                                                    ALU.mult, ALU.add)
                link(last)
                norm_stats(x1, w)
            for b in range(NB):
                norm_apply(hrow, x1, tiles(b), s_hn, 5 + b)
            dve.wait_ge(s_scT, 1)
            link(dve.tensor_copy(score2[:, :].rearrange("p (t r) -> p r t", r=2),
                                 bank[5][:, 0:256].rearrange("p (r t) -> p r t", r=2)))

            thr, cand, inc = ibits[:, 0:1], ibits[:, 1:2], ibits[:, 2:3]
            dve.memset(thr, 0)
            link(dve.memset(cand, 1 << (BITS - 1)))

            def shared_chunk(n):
                dve.wait_ge(s_shsil, n + 1)
                if n:
                    dve.wait_ge(s_shout, n)
                for t in range(SHT):
                    last = dve.tensor_tensor(sh_hid[:, t, :], bank[2 + t][:, :], sgate[:, t, :], ALU.mult)
                last.then_inc(s_shhid, 1)

            def shared_add(n):
                dve.wait_ge(s_shout, n + 1)
                dve.tensor_tensor(x1[:, 4 * n:4 * n + 4, :].rearrange("p i c -> p (i c)"), bank[4][:, :],
                                  x1[:, 4 * n:4 * n + 4, :].rearrange("p i c -> p (i c)"), ALU.add).then_inc(s_base, 1)

            for it in range(BITS):
                bit = BITS - 1 - it
                dve.tensor_scalar(junk[:, :], score2[:, :], cand.bitcast(F32), 0.0, ALU.is_ge, ALU.add,
                                  accum_out=cnt[:, 0:1]).then_inc(s_cnt, 1)
                if it >= 6 and (it - 6) % 6 == 0 and (it - 6) // 6 < 4:
                    shared_chunk((it - 6) // 6)
                if it >= 9 and (it - 9) % 6 == 0 and (it - 9) // 6 < 4:
                    shared_add((it - 9) // 6)
                dve.wait_ge(s_tot, it + 1)
                link(dve.tensor_scalar(inc, bank[5][:, 511:512], float(CAP), float(1 << bit), ALU.is_ge, ALU.mult))
                if bit:
                    dve.scalar_tensor_tensor(cand, inc, 1 << (bit - 1), thr, ALU.bitwise_or, ALU.bitwise_or)
                link(dve.tensor_tensor(thr, thr, inc, ALU.bitwise_or))

            gt, eq, scan, chosen, pos = (sel[:, k, :] for k in range(5))
            thr_f = thr.bitcast(F32)
            dve.tensor_scalar(gt, score2[:, :], thr_f, 0.0, ALU.is_gt, ALU.add, accum_out=cnt[:, 1:2])
            dve.tensor_scalar(eq, score2[:, :], thr_f, 0.0, ALU.is_equal, ALU.add,
                              accum_out=cnt[:, 2:3]).then_inc(s_cnt, 1)
            dve.wait_ge(s_cnt, BITS + 1)
            link(dve.tensor_tensor_scan(scan, eq, eq, 0.0, ALU.add, ALU.max))
            dve.wait_ge(s_tot, BITS + 1)
            link(dve.tensor_scalar(rneed[:, :], bank[5][:, 511:512], -1.0, float(CAP), ALU.mult, ALU.add))
            link(dve.scalar_tensor_tensor(eq, scan, rneed[:, :], eq, ALU.is_le, ALU.mult))
            dve.scalar_tensor_tensor(chosen, eq, 1.0, gt, ALU.mult, ALU.add, accum_out=cnt[:, 3:4]).then_inc(s_cnt, 1)
            dve.wait_ge(s_cnt, BITS + 2)
            link(dve.tensor_tensor_scan(scan, chosen, chosen, 0.0, ALU.add, ALU.max))
            dve.wait_ge(s_tot, BITS + 2)
            dve.scalar_tensor_tensor(pos, scan, bank[5][:, 511:512], chosen, ALU.add, ALU.mult).then_inc(s_pos, 1)
            dve.wait_ge(s_posT, 1)
            link(dve.tensor_scalar(slot_i[:, 0, :].rearrange("p (r k e) -> p r k e", r=2, k=BLK),
                                   bank[5][:, 0:256].rearrange("p (r e k) -> p r k e", r=2, k=BLK),
                                   -1.0, None, ALU.add))
            dve.tensor_scalar(slot_i[:, 1, :], slot_i[:, 0, :], 4, None, ALU.arith_shift_right)
            link(dve.tensor_scalar(slot_i[:, 2, :], slot_i[:, 0, :], HI - 1, None, ALU.bitwise_and))
            link(dve.tensor_copy(slot_h[:, :, :], slot_i[:, 1:3, :]))
            for a in range(HI):
                dve.tensor_scalar(one_hi[:, :, a, :], slot_h[:, 0, :].rearrange("p (n e) -> p n e", e=8), float(a), None, ALU.is_equal)
            for a in range(HI):
                last = dve.tensor_scalar(one_lo[:, :, a, :], slot_h[:, 1, :].rearrange("p (n e) -> p n e", e=8), float(a), None, ALU.is_equal)
            link(last)
            dve.tensor_tensor(one_lo[:, :, :, :], one_lo[:, :, :, :],
                              token_no[:, :].rearrange("p (n e) -> p n e", e=8).unsqueeze(2).to_broadcast([P, 32, HI, 8]),
                              ALU.mult).then_inc(s_hot, 1)
            dve.wait_ge(s_tab, 1)
            link(dve.tensor_tensor(ext[:, :].rearrange("p (b e) -> p b e", e=8),
                                   bank[5][:, 0:256].rearrange("p (b e) -> p b e", e=8),
                                   pick[:, :].unsqueeze(1).to_broadcast([P, 32, 8]), ALU.mult))
            dve.tensor_reduce(itab[:, :], ext[:, :].rearrange("p (b e) -> p b e", e=8), AX.X, ALU.add).then_inc(s_itab, 1)
            dve.wait_ge(s_itT, 1)
            dve.tensor_copy(itabT[:, :], bank[5][0:HI, 0:256]).then_inc(s_itTe, 1)
            dve.wait_ge(s_spread, 1)
            link(dve.tensor_tensor(ext[:, :].rearrange("p (g e a) -> p g e a", g=4, e=8),
                                   bank[5][:, 256:512].rearrange("p (g a e) -> p g e a", g=4, e=8),
                                   pick[:, :].unsqueeze(1).unsqueeze(1).to_broadcast([P, 4, 8, 8]), ALU.mult))
            dve.tensor_reduce(rows[:, :, :, :].rearrange("p g c e -> p (g c e)"),
                              ext[:, :].rearrange("p (m a) -> p m a", a=8), AX.X, ALU.add).then_inc(s_rows, 1)

            def keep_x(e):
                dve.wait_ge(s_xsT, e + 1)
                if e >= 2:
                    dve.wait_ge(s_gu, FT * (e - 1))
                dve.tensor_copy(xselT[:, e % 2, :], bank[5][:, 0:CAP]).then_inc(s_xs, 1)

            def add_bias(e):
                dve.wait_ge(s_dn, e + 1)
                if e >= 2:
                    dve.wait_ge(s_scat, 16 * CH * (e - 1))
                dve.tensor_tensor(eo[:, e % 2, :, :], bank[3 + e % 2][:, 0:CAP].rearrange("p (c d) -> p c d", c=CH),
                                  down_b_bc[:, e, :].unsqueeze(1).to_broadcast([P, CH, C]), ALU.add).then_inc(s_eb, 1)

            dve.wait_ge(s_db_in, 16)
            keep_x(0)
            for q in range(E * FT):
                e, j = divmod(q, FT)
                dve.wait_ge(s_sil, q + 1)
                if e >= 2:
                    dve.wait_ge(s_dn, e - 1)
                dve.scalar_tensor_tensor(hidden[:, e % 2, j, :], bank[q % 3][:, 0:CAP], biasT[:, 0, j, e:e + 1],
                                         sgate[:, q % 2, 0:CAP], ALU.add, ALU.mult).then_inc(s_hid, 1)
                if j == 1 and e > 0:
                    add_bias(e - 1)
                if j == 2 and e + 1 < E:
                    keep_x(e + 1)
            add_bias(E - 1)

        @block.tensor
        def _(pe):
            done_w = [0]

            def turn_weights(n):
                for _ in range(n):
                    k = done_w[0]
                    done_w[0] += 1
                    kind = k % KINDS
                    pe.wait_ge(s_raw[k % RING], 16 * (k // RING + 1))
                    if k >= 2:
                        pe.wait_ge(s_wT, k - 1)
                    for j in range(FT):
                        src = raw[:, k % RING, j:F:FT] if kind == 2 else raw[:, k % RING, j * P:(j + 1) * P]
                        last = pe.transpose(bank[6 + k % 2][:, j * P:(j + 1) * P], src, ident[:, :])
                    last.then_inc(s_wTp, 1)

            def first(o):
                return o == 0

            pe.wait_ge(s_ident, 1)
            pe.wait_ge(s_small_in, 16 * 7)
            pe.transpose(bank[5][:, 0:16], filt_rows[:, :], ident[0:16, 0:16])
            pe.transpose(bank[5][:, 16:32], gate_rows[:, :], ident[0:E, 0:E])
            for k in range(2):
                for j in range(FT):
                    o = 32 + (k * FT + j) * E
                    last = pe.transpose(bank[5][:, o:o + E], bias_rows[:, k, j:F:FT], ident[0:E, 0:E])
            last.then_inc(s_constT, 1)
            pe.wait_ge(s_sh_in, 48)
            for t in range(6):
                o = bank[4][:, t * P:(t + 1) * P] if t < 4 else bank[5][:, 256 + (t - 4) * P:256 + (t - 3) * P]
                if t == 4:
                    pe.wait_ge(s_const, 1)
                last = pe.transpose(o, sh_raw[:, t, :], ident[:, :])
            last.then_inc(s_shT, 1)
            turn_weights(FILL["start"])
            for b in range(NB):
                for r in range(2):
                    pe.wait_ge(s_xn, 2 * b + 2)
                    for k in range(BPB):
                        last = pe.transpose(bank[2 * b + r][:, k * P:(k + 1) * P], xn_tok[:, 2 * (b * BPB + k) + r, :],
                                            ident[:, :])
                    last.then_inc(s_xnT, 1)
            turn_weights(FILL["lift"])
            pe.wait_ge(s_diag, 1)
            for b in range(NB):
                pe.wait_ge(s_xp, 4)
                for k, (r, o) in enumerate(((1, 0), (0, 1), (1, 1), (0, 2))):
                    last = pe.matmul(bank[b][:, :], diag[:, k, :], xp[:, r, b, o:o + N1], start=(k == 0), stop=(k == 3))
                last.then_inc(s_h1, 1)
            turn_weights(FILL["band"])
            pe.wait_ge(s_l1, NB)
            pe.wait_ge(s_h1e, 1)
            for k in range(4):
                last = pe.matmul(bank[0][:, :], diag[:, k, :], l1p[:, :, k:k + N1:2], start=(k == 0), stop=(k == 3))
            last.then_inc(s_h2, 1)
            pe.wait_ge(s_l2, 1)
            pe.wait_ge(s_h1e, 2)
            for k in range(4):
                last = pe.transpose(bank[1][:, k * P:(k + 1) * P], l2f[:, k * P:(k + 1) * P], ident[:, :])
            last.then_inc(s_qvT, 1)
            pe.wait_ge(s_q, 1)
            for k in range(4):
                last = pe.transpose(bank[2][:, k * P:(k + 1) * P], qf[:, k * P:(k + 1) * P], ident[:, :])
            last.then_inc(s_qvT, 1)
            pe.wait_ge(s_shw, 1)
            pe.wait_ge(s_h2e, 1)
            TAPS = ((0, ((0, 0), (1, 1), (2, 2))), (1, ((3, 1), (4, 2))))
            for par, taps_of in TAPS:
                for k, o in taps_of:
                    pe.matmul(bank[4 + par][:, :], diag[:, 9 + k, :], h2p[:, :, o:o + N2], start=(k in (0, 3)), stop=False,
                              skip_group_check=True)
            pe.wait_ge(s_qve, 2)
            for b in range(NB):
                for k in range(2):
                    o = (2 * b + k) * P
                    last = pe.matmul(bank[3][:, b * P:(b + 1) * P], kT[:, o:o + P], vT[:, o:o + P],
                                     start=(k == 0), stop=(k == 1))
            last.then_inc(s_kv, 1)
            pe.wait_ge(s_kvm, 1)
            for b in range(NB):
                o = slice(b * N2, (b + 1) * N2)
                pe.matmul(bank[1][:, o], kvz[:, 1, b, :], qf[:, o], start=True, stop=True)
                last = pe.matmul(bank[2][:, o], kvz[:, 0, b, :], qf[:, o], start=True, stop=True)
            last.then_inc(s_nd, 1)
            turn_weights(FILL["attn"])
            pe.wait_ge(s_attn, 1)
            for par, taps_of in TAPS:
                for k, o in taps_of:
                    last = pe.matmul(bank[4 + par][:, :], diag[:, 4 + k, :], ap_[:, :, o:o + N2], start=False,
                                     stop=(o == 2), skip_group_check=True)
            last.then_inc(s_up2, 1)
            def synth(n, band, d0, begin):
                for t in range(4):
                    i = 4 * n + t
                    blk, par = divmod(i, 2)
                    b, m0 = blk // BPB, (blk % BPB) * P
                    for k, o in TAPS[par][1]:
                        last = pe.matmul(bank[n][:, t * P:(t + 1) * P], band[:, b, m0 + o:m0 + o + P], diag[:, d0 + k, :],
                                         start=(begin and t == 0 and k == 0), stop=(not begin and o == 2),
                                         skip_group_check=True)
                return last

            for n in range(4):
                synth(n, h1p, 9, True)
            pe.wait_ge(s_r1, 2)
            for n in range(4):
                synth(n, r1p, 4, False).then_inc(s_up1, 1)
            turn_weights(FILL["up"])
            turn_weights(FILL["norm"])
            for n in range(4):
                pe.wait_ge(s_hn, n + 1)
                for t in range(4):
                    last = pe.transpose(bank[n][:, t * P:(t + 1) * P], hrow[:, 4 * n + t, 0:C], ident[:, :])
                last.then_inc(s_hTp, 1)
            pe.wait_ge(s_r1, 2)
            for i in range(NT):
                pe.wait_ge(s_hT, i // 4 + 1)
                blk, par = divmod(i, 2)
                o = par * P + blk
                last = pe.matmul(bank[4][:, o:par * P + P:BLK], hT[:, i, :], gate_wT, start=True, stop=True)
            last.then_inc(s_logit, 1)
            pe.wait_ge(s_score, 1)
            for r in range(2):
                last = pe.transpose(bank[5][:, r * P:(r + 1) * P], sel[:, 0, r * P:(r + 1) * P], ident[:, :])
            last.then_inc(s_scT, 1)
            pe.wait_ge(s_masks, 1)

            def count(n, *pairs):
                pe.wait_ge(s_cnt, n)
                for k, (mask, col) in enumerate(pairs):
                    last = pe.matmul(bank[5][:, 511:512], mask[:, :], cnt[:, col:col + 1], start=(k == 0),
                                     stop=(k == len(pairs) - 1))
                last.then_inc(s_tot, 1)

            def shared_up(n, t):
                if n:
                    pe.wait_ge(s_shhid, n)
                    pe.wait_ge(s_shsil, n)
                rhs = hT[:, 4 * n:4 * n + 4, :].rearrange("p i t -> p (i t)")
                pe.matmul(bank[t][:, :], sh_wT[:, t, :], rhs, start=True, stop=True)
                last = pe.matmul(bank[2 + t][:, :], sh_wT[:, 2 + t, :], rhs, start=True, stop=True)
                if t == 1:
                    last.then_inc(s_shgu, 1)

            def shared_down(n):
                pe.wait_ge(s_shhid, n + 1)
                if n:
                    pe.wait_ge(s_base, n)
                for t in range(4):
                    for k in range(SHT):
                        last = pe.matmul(bank[4][:, t * P:(t + 1) * P], sh_hid[:, k, t * P:(t + 1) * P], sh_wT[:, 4 + k, :],
                                         start=(k == 0), stop=(k == SHT - 1))
                last.then_inc(s_shout, 1)

            pe.wait_ge(s_scT, 1)
            for it in range(BITS):
                count(it + 1, (same8_bf, 0))
                if it < 24:
                    n, ph = divmod(it, 6)
                    if ph == 3:
                        shared_up(n, 0)
                    if ph == 4:
                        shared_up(n, 1)
                if it >= 7 and (it - 7) % 6 == 0 and (it - 7) // 6 < 4:
                    shared_down((it - 7) // 6)
                if it in TURNS:
                    turn_weights(TURNS[it])
            count(BITS + 1, (same8_bf, 1), (earlier, 2))
            count(BITS + 2, (earlier, 3))
            pe.wait_ge(s_pos, 1)
            for r in range(2):
                last = pe.transpose(bank[5][:, r * P:(r + 1) * P], sel[:, 4, r:256:2], ident[:, :])
            last.then_inc(s_posT, 1)
            pe.wait_ge(s_hot, 1)
            for g in range(2):
                for i in range(NT):
                    n = 2 * i + g
                    last = pe.matmul(bank[5][:, g * P:(g + 1) * P], one_hi[:, n, :, :].rearrange("p a e -> p (a e)"),
                                     one_lo[:, n, :, :].rearrange("p b e -> p (b e)"), start=(i == 0), stop=(i == NT - 1))
            last.then_inc(s_tab, 1)
            pe.wait_ge(s_itab, 1)
            for g in range(2):
                last = pe.transpose(bank[5][0:HI, g * P:(g + 1) * P], itab[:, g * HI:(g + 1) * HI], ident[:, :])
            last.then_inc(s_itT, 1)
            pe.wait_ge(s_itTe, 1)
            pe.matmul(bank[5][:, 256:512], sel_lo[:, :], itabT[:, :], start=True, stop=True).then_inc(s_spread, 1)

            def turn_x(e):
                pe.wait_ge(s_gath[e % 3], 16 * CH * (e // 3 + 1))
                if e == 0:
                    pe.wait_ge(s_rows, 1)
                else:
                    pe.wait_ge(s_xs, e)
                for c in range(CH):
                    last = pe.transpose(bank[5][:, c * P:(c + 1) * P], gath[:, e % 3, c, 0:C], ident[:, :])
                last.then_inc(s_xsT, 1)

            def down(q):
                e, j = divmod(q, FT)
                pe.wait_ge(s_hid, q + 1)
                if j == 0 and e >= 2:
                    pe.wait_ge(s_eb, e - 1)
                for c in range(CH):
                    last = pe.matmul(bank[3 + e % 2][:, c * P:(c + 1) * P], hidden[:, e % 2, j, c * P:(c + 1) * P],
                                     wT[:, e, 2, j, :], start=(j == 0 and c == 0), stop=(j == FT - 1),
                                     skip_group_check=True)
                if j == FT - 1:
                    last.then_inc(s_dn, 1)

            pe.wait_ge(s_wT, GROUPS)
            pe.wait_ge(s_base, 4)
            turn_x(0)
            for q in range(E * FT):
                e, j = divmod(q, FT)
                if j == 0:
                    pe.wait_ge(s_xs, e + 1)
                if q >= 3:
                    pe.wait_ge(s_hid, q - 2)
                pe.matmul(bank[q % 3][:, 0:CAP], wT[:, e, 0, j, :], xselT[:, e % 2, :], start=True, stop=True)
                pe.matmul(bank[q % 3][:, CAP:2 * CAP], wT[:, e, 1, j, :], xselT[:, e % 2, :], start=True,
                          stop=True).then_inc(s_gu, 1)
                if q >= 2:
                    down(q - 2)
                if j == 1 and e + 1 < E:
                    turn_x(e + 1)
            down(E * FT - 2)
            down(E * FT - 1)


_INS = ['L0_attn_x', 'L0_attn_h_filter', 'L0_attn_g_filter', 'L0_attn_h_synth', 'L0_attn_g_synth',
        'L0_attn_norm_gamma', 'L0_attn_norm_beta', 'L0_ffn_gate_w', 'L0_ffn_up_w', 'L0_ffn_up_b', 'L0_ffn_gw',
        'L0_ffn_gb', 'L0_ffn_down_w', 'L0_ffn_down_b', 'L0_ffn_sh_gate_w', 'L0_ffn_sh_up_w', 'L0_ffn_sh_down_w']
_OUTS = [((2, 1024, 128), 'float32')]


def kernel(**inputs):
    import numpy as _np
    import concourse.bacc as _bacc
    from concourse import mybir as _mybir
    from concourse.bass_utils import run_bass_kernel_spmd as _run

    nc = _bacc.Bacc("TRN2", target_bir_lowering=False, num_devices=1)
    arrays, args = {}, []
    for name in _INS:
        a = _np.ascontiguousarray(inputs[name])
        arrays[f"in_{name}_dram"] = a
        args.append(nc.dram_tensor(f"in_{name}_dram", a.shape, _mybir.dt.from_np(a.dtype), kind="ExternalInput").ap())
    for i, (shape, dtype) in enumerate(_OUTS):
        dt = _mybir.dt.from_np(_np.dtype(dtype))
        args.append(nc.dram_tensor(f"out_{i}_dram", shape, dt, kind="ExternalOutput").ap())
    wavelet_attention_moe(nc, *args)
    r = _run(nc, [arrays], core_ids=[0])
    return r.results[0]["out_0_dram"]
```

```python
from contextlib import ExitStack

import concourse.bass as bass
from concourse import mybir

ALU = mybir.AluOpType
ACT = mybir.ActivationFunctionType
AX = mybir.AxisListType
F32 = mybir.dt.float32
F16 = mybir.dt.float16
BF16 = mybir.dt.bfloat16
I32 = mybir.dt.int32
U32 = mybir.dt.uint32

P = 128
LN_EPS = 1e-5
ATTN_EPS = 1e-6
HEAD = 8


def wavelet_attention_moe(nc, x, packed, weights, shared, down_b, out):
    NB, SEQ, C = x.shape
    TOK = NB * SEQ
    E, _, KINDS, FT, _ = weights.shape
    SHT = shared.shape[1] // KINDS
    CAP = -(-TOK * 2 // E)
    BLK = TOK // 256
    BPB = BLK // NB
    NT = TOK // P
    N1, N2 = SEQ // 2, SEQ // 4
    ROW = C + E
    GBUF = 6
    CH = CAP // P
    BITS = 30
    HI = 16

    h_rows = nc.dram_tensor("h_rows", [TOK, ROW], F32)

    ctx = ExitStack()
    with ctx:
        ctx.enter_context(nc.allow_low_precision(reason="exact integers"))

        def sb(name, shape, dt=F32):
            return ctx.enter_context(nc.sbuf_tensor(name, shape, dt))

        def sem(name):
            return ctx.enter_context(nc.semaphore(name))

        bank = [ctx.enter_context(nc.psum_tensor(f"bank{i}", [P, 512], F32)) for i in range(8)]

        ident = sb("ident", [P, P])
        same8 = sb("same8", [P, P])
        same8_bf = sb("same8_bf", [P, P], BF16)
        earlier = sb("earlier", [P, P], BF16)
        pick = sb("pick", [P, 8])
        sel_lo = sb("sel_lo", [HI, P])
        token_no = sb("token_no", [P, 2 * P], F16)
        half_pow = sb("half_pow", [P, NT])
        consts = sb("consts", [P, packed.shape[1]])
        taps = consts[:, 0:16]
        gate_wT = consts[:, 16:32]
        biasT = consts[:, 32:160].rearrange("p (k j e) -> p k j e", k=2, j=FT)
        gamma_bc = consts[:, 160:160 + C]
        beta_bc = consts[:, 160 + C:160 + 2 * C]
        comb = sb("comb", [P, 2, 3])
        diag = sb("diag", [P, 14, P])
        sh_wT = sb("sh_wT", [P, 6, P])

        x_tok = sb("x_tok", [P, NT, C])
        x1 = sb("x1", [P, NT, C])
        hrow = sb("hrow", [P, NT, ROW])
        hT = sb("hT", [P, NT, P])
        wT = sb("wT", [P, E, KINDS, FT, P])

        area = sb("area", [P, 2048 + 4 * 514 + 2 * 516 + 2 * 514 * 2 + 4 * 258])
        at = [0]

        def carve(n, base=None):
            if base is not None:
                at[0] = base
            a = area[:, at[0]:at[0] + n]
            at[0] += n
            return a

        xn_tok = carve(2048, 0).rearrange("p (i c) -> p i c", i=NT)
        xp = carve(4 * 514).rearrange("p (r b n) -> p r b n", r=2, b=NB)
        l1p = carve(2 * 516).rearrange("p (b n) -> p b n", b=NB)
        h1p = carve(2 * 514).rearrange("p (b n) -> p b n", b=NB)
        r1p = carve(2 * 514).rearrange("p (b n) -> p b n", b=NB)
        h2p = carve(2 * 258).rearrange("p (b n) -> p b n", b=NB)
        ap_ = carve(2 * 258).rearrange("p (b n) -> p b n", b=NB)
        one_hi = carve(2048, 0).bitcast(F16).rearrange("p (n a e) -> p n a e", a=HI, e=8)
        one_lo = carve(2048).bitcast(F16).rearrange("p (n b e) -> p n b e", b=HI, e=8)
        sel = carve(5 * 256).rearrange("p (k n) -> p k n", k=5)
        sh_hid = carve(2 * 512).rearrange("p (t n) -> p t n", t=2)
        slot_i = carve(3 * 256).bitcast(I32).rearrange("p (k n) -> p k n", k=3)
        slot_h = carve(256).bitcast(F16).rearrange("p (k n) -> p k n", k=2)
        ext = carve(256)
        score2 = carve(256)
        gath = carve(GBUF * CH * ROW, 0).rearrange("p (s c r) -> p s c r", s=GBUF, c=CH)
        xselT = carve(2 * CAP, 4104).rearrange("p (s n) -> p s n", s=2)
        hidden = carve(2 * FT * CAP).rearrange("p (s j n) -> p s j n", s=2, j=FT)
        eo = carve(2 * CH * C).rearrange("p (s c d) -> p s c d", s=2, c=CH)
        flat_hT = hT[:, :, :].rearrange("p i t -> p (i t)")
        flat_hrow = hrow[:, :, :].rearrange("p i t -> p (i t)")
        l2f, expf, qf, vT = (flat_hT[:, 512 * k:512 * k + 512] for k in range(4))
        kT, den = (flat_hrow[:, 512 * k:512 * k + 512] for k in range(2))
        kvz = x1[:, 8:12, :].rearrange("p (z b) c -> p z b c", z=2)
        down_b_bc = x_tok
        junk = sb("junk", [P, 256], BF16)
        sgate = sb("sgate", [P, 2, 512])
        SGB = 1024 // CAP
        sgate_e = sgate[:, :, :].rearrange("p t n -> p (t n)").rearrange("p (s n) -> p s n", n=CAP)
        UP_BANKS = [bank[i] for i in (0, 1, 2, 6, 7)]

        def up_bank(q):
            return UP_BANKS[q % len(UP_BANKS)]

        stats = sb("stats", [P, NT, 6])
        small = sb("small", [P, 8, NT])
        zsum = sb("zsum", [P, 2])
        cnt = sb("cnt", [P, 4], BF16)
        ibits = sb("ibits", [P, 4], I32)
        rneed = sb("rneed", [P, 1])
        itab = sb("itab", [P, 32])
        itabT = sb("itabT", [HI, 256])
        rows = sb("rows", [P, 2, CH, 8], U32)

        s_x = [sem(f"s_x{b}") for b in range(NB)]
        s_db_in = sem("s_db_in")
        s_wT = [sem(f"s_wT{e}") for e in range(E)]
        s_shw = sem("s_shw")
        s_ident = sem("s_ident")
        s_pool = sem("s_pool")
        s_masks = sem("s_masks")
        s_diag = sem("s_diag")
        s_comb = sem("s_comb")
        s_xb = sem("s_xb")
        s_var = sem("s_var")
        s_rstd = sem("s_rstd")
        s_const = sem("s_const")
        s_pad = sem("s_pad")
        s_xn = sem("s_xn")
        s_xnT = sem("s_xnT")
        s_xp = sem("s_xp")
        s_l1 = sem("s_l1")
        s_l2 = sem("s_l2")
        s_h1 = sem("s_h1")
        s_h1e = sem("s_h1e")
        s_h2 = sem("s_h2")
        s_h2e = sem("s_h2e")
        s_exp = sem("s_exp")
        s_q = sem("s_q")
        s_qvT = sem("s_qvT")
        s_qve = sem("s_qve")
        s_kv = sem("s_kv")
        s_kvm = sem("s_kvm")
        s_nd = sem("s_nd")
        s_attn = sem("s_attn")
        s_up2 = sem("s_up2")
        s_r1 = sem("s_r1")
        s_up1 = sem("s_up1")
        s_t = sem("s_t")
        s_hn = sem("s_hn")
        s_hTp = sem("s_hTp")
        s_hT = sem("s_hT")
        s_logit = sem("s_logit")
        s_score = sem("s_score")
        s_scT = sem("s_scT")
        s_hrow = sem("s_hrow")
        s_hstore = sem("s_hstore")
        s_cnt = sem("s_cnt")
        s_tot = sem("s_tot")
        s_shg = sem("s_shg")
        s_shu = sem("s_shu")
        s_shsil = sem("s_shsil")
        s_shhid = sem("s_shhid")
        s_shout = sem("s_shout")
        s_base = sem("s_base")
        s_store = sem("s_store")
        s_need = sem("s_need")
        s_pos = sem("s_pos")
        s_posT = sem("s_posT")
        s_hot = sem("s_hot")
        s_tab = sem("s_tab")
        s_itab = sem("s_itab")
        s_itT = sem("s_itT")
        s_itTe = sem("s_itTe")
        s_spread = sem("s_spread")
        s_rows = sem("s_rows")
        s_gath = [sem(f"s_gath{i}") for i in range(GBUF)]
        s_xsT = sem("s_xsT")
        s_xs = sem("s_xs")
        s_gu = sem("s_gu")
        s_sil = sem("s_sil")
        s_hid = sem("s_hid")
        s_dn = sem("s_dn")
        s_eb = sem("s_eb")
        s_eo = sem("s_eo")
        s_scat = sem("s_scat")
        s_dve = sem("s_dve")
        s_act = sem("s_act")

        x_v = x.rearrange("b (k p r) c -> p (b k) (r c)", p=P, r=2)
        out_v = out.rearrange("b (k p r) c -> p (b k) (r c)", p=P, r=2)
        out_rows = out.rearrange("b s c -> (b s) c")
        h_v = h_rows[:, :].rearrange("(k p r) c -> p k (r c)", p=P, r=2)

        def tiles(b):
            return slice(b * NT // NB, (b + 1) * NT // NB)

        def fill(it, plan):
            for at_step, do in plan.items():
                n, off = divmod(it - at_step, 6)
                if off == 0 and 0 <= n < NT // 4:
                    do(n)

        block = ctx.enter_context(nc.Block())

        @block.sync
        def _(sp):
            def load_x(b):
                sp.dma_start(x_tok[:, tiles(b), :].rearrange("p (k r) c -> p k (r c)", r=2),
                             x_v[:, b * BPB:(b + 1) * BPB, :]).then_inc(s_x[b], 16)

            load_x(0)
            sp.dma_start(consts[:, :], packed).then_inc(s_const, 16)
            load_x(1)
            sp.dma_start(sh_wT[:, :, :], shared).then_inc(s_shw, 16)
            for e in range(E):
                sp.dma_start(wT[:, e, :, :, :], weights[e]).then_inc(s_wT[e], 16)
            for b in range(NB):
                sp.wait_ge(s_hn, 2 * (b + 1))
                sp.wait_ge(s_hrow, 1)
                sp.dma_start(h_v[:, b * BPB:(b + 1) * BPB, :],
                             hrow[:, tiles(b), :].rearrange("p (k r) c -> p k (r c)", r=2)).then_inc(s_hstore, 16)
            sp.dma_start(down_b_bc[:, :, :].rearrange("p e c -> p (e c)"),
                         down_b.rearrange("e c -> (e c)").partition_broadcast(P)).then_inc(s_db_in, 16)
            for n in range(NT // 4):
                sp.wait_ge(s_base, n + 1)
                sp.dma_start(out_v[:, 2 * n:2 * n + 2, :],
                             x1[:, 4 * n:4 * n + 4, :].rearrange("p (k r) c -> p k (r c)", r=2)).then_inc(s_store, 16)
            sp.wait_ge(s_hstore, 16 * NB)
            sp.wait_ge(s_store, 16 * (NT // 4))
            sp.wait_ge(s_scat, 16 * CH * E)

        @block.gpsimd
        def _(pool):
            step = [0]

            def link(ins):
                step[0] += 1
                ins.then_inc(s_pool, 1)
                pool.wait_ge(s_pool, step[0])

            link(pool.memset(ident[:, :], 0.0))
            pool.affine_select(out=ident[:, :], in_=ident[:, :], compare_op=ALU.not_equal, fill=1.0, base=0,
                               pattern=[[-1, P]], channel_multiplier=1).then_inc(s_ident, 1)
            pool.memset(half_pow[:, :], -0.5)
            pool.memset(xp[:, :, :, 0:1], 0.0)
            pool.memset(xp[:, :, :, N1 + 1:N1 + 2], 0.0)
            pool.memset(l1p[:, :, 0:1], 0.0)
            pool.memset(l1p[:, :, N1 + 1:N1 + 4], 0.0)
            for band, n in ((h1p, N1), (r1p, N1), (h2p, N2), (ap_, N2)):
                pool.memset(band[:, :, 0:1], 0.0)
                last = pool.memset(band[:, :, n + 1:n + 2], 0.0)
            last.then_inc(s_pad, 1)
            link(pool.memset(same8[:, :], 1.0))
            link(pool.affine_select(out=same8[:, :], in_=same8[:, :], compare_op=ALU.is_ge, fill=0.0, base=0,
                                    pattern=[[-8, 16], [0, 8]], channel_multiplier=1))
            link(pool.affine_select(out=same8[:, :], in_=same8[:, :], compare_op=ALU.is_ge, fill=0.0, base=7,
                                    pattern=[[8, 16], [0, 8]], channel_multiplier=-1))
            pool.tensor_copy(same8_bf[:, :], same8[:, :])
            pool.affine_select(out=earlier[:, :], in_=same8[:, :], compare_op=ALU.is_ge, fill=0.0, base=-1,
                               pattern=[[1, P]], channel_multiplier=-1)
            link(pool.memset(sel_lo[:, :], 1.0))
            link(pool.affine_select(out=sel_lo[:, :], in_=sel_lo[:, :], compare_op=ALU.is_ge, fill=0.0, base=0,
                                    pattern=[[1, P]], channel_multiplier=-8))
            link(pool.affine_select(out=sel_lo[:, :], in_=sel_lo[:, :], compare_op=ALU.is_ge, fill=0.0, base=7,
                                    pattern=[[-1, P]], channel_multiplier=8))
            pool.iota(token_no[:, :], pattern=[[1, 2], [256, BLK], [0, E]], base=0, channel_multiplier=2,
                      allow_small_or_imprecise_dtypes=True).then_inc(s_masks, 1)

            def rsqrt(n, w):
                pool.wait_ge(s_var, n + 1)
                v = small[:, 5, w]
                link(pool.tensor_scalar(v, v, LN_EPS, None, ALU.add))
                pool.tensor_tensor(small[:, 6, w], v, half_pow[:, w], ALU.pow).then_inc(s_rstd, 1)

            rsqrt(0, tiles(0))
            rsqrt(1, tiles(1))
            pool.wait_ge(s_const, 16)
            pool.wait_ge(s_xn, 2 * NB)
            pool.tensor_tensor(x_tok[:, :, :], x_tok[:, :, :],
                               beta_bc[:, :].unsqueeze(1).to_broadcast([P, NT, C]), ALU.add).then_inc(s_xb, 1)
            for n in range(2, 6):
                rsqrt(n, tiles(n % 2))

            def gather(e):
                g, k = divmod(e, 8)
                if e >= GBUF:
                    pool.wait_ge(s_eo, CH * (e - GBUF + 1))
                for c in range(CH):
                    pool.indirect_dma_start(out=gath[:, e % GBUF, c, :], out_offset=None, in_=h_rows[:, :],
                                            in_offset=bass.IndirectOffsetOnAxis(ap=rows[:, g, c, k:k + 1], axis=0),
                                            ).then_inc(s_gath[e % GBUF], 16)

            def scatter(e):
                g, k = divmod(e, 8)
                pool.wait_ge(s_eo, CH * (e + 1))
                if e == 0:
                    pool.wait_ge(s_store, 16 * (NT // 4))
                else:
                    pool.wait_ge(s_scat, 16 * CH * e)
                for c in range(CH):
                    pool.indirect_dma_start(out=out_rows, in_=eo[:, e % 2, c, :], in_offset=None,
                                            out_offset=bass.IndirectOffsetOnAxis(ap=rows[:, g, c, k:k + 1], axis=0),
                                            compute_op=ALU.add).then_inc(s_scat, 16)

            pool.wait_ge(s_rows, 1)
            pool.wait_ge(s_hstore, 16 * NB)
            for e in range(GBUF - 1):
                gather(e)
            for e in range(E):
                if e + GBUF - 1 < E:
                    gather(e + GBUF - 1)
                scatter(e)

        def weigh(act, e):
            act.wait_ge(s_eb, e + 1)
            for c in range(CH):
                act.activation(eo[:, e % 2, c, :], eo[:, e % 2, c, :], ACT.Copy,
                               scale=gath[:, e % GBUF, c, C + e:C + e + 1]).then_inc(s_eo, 1)

        @block.scalar
        def _(act):
            act.wait_ge(s_pad, 1)
            for b in range(NB):
                for r in range(2):
                    act.wait_ge(s_xnT, 2 * b + r + 1)
                    act.copy(xp[:, r, b, 1:N1 + 1], bank[2 * b + r][:, :]).then_inc(s_xp, 1)
            for b in range(NB):
                act.wait_ge(s_h1, b + 1)
                act.copy(h1p[:, b, 1:N1 + 1], bank[b][:, :]).then_inc(s_h1e, 1)
            act.wait_ge(s_h2, 1)
            act.copy(h2p[:, :, 1:N2 + 1], bank[0][:, :].rearrange("p (b n) -> p b n", b=NB)).then_inc(s_h2e, 1)
            act.wait_ge(s_l2, 1)
            act.activation(expf[:, :], l2f[:, :], ACT.Exp).then_inc(s_exp, 1)
            act.wait_ge(s_qvT, 1)
            act.copy(vT[:, :], bank[1][:, :]).then_inc(s_qve, 1)
            act.wait_ge(s_up2, 1)
            act.copy(r1p[:, :, 2:N1 + 2:2], bank[5][:, :].rearrange("p (b n) -> p b n", b=NB)).then_inc(s_r1, 1)
            for n in range(4):
                act.wait_ge(s_hTp, n + 1)
                act.copy(hT[:, 4 * n:4 * n + 4, :].rearrange("p i t -> p (i t)"), bank[n][:, :]).then_inc(s_hT, 1)
            act.wait_ge(s_logit, 1)
            act.activation(sel[:, 0, :], bank[4][:, 0:256], ACT.Sigmoid).then_inc(s_score, 1)
            act.wait_ge(s_score, 1)
            act.copy(hrow[:, :, C:ROW].rearrange("p (k r) e -> p k r e", r=2),
                     sel[:, 0, :].rearrange("p (r e k) -> p k r e", r=2, e=E)).then_inc(s_hrow, 1)
            for n in range(4):
                for t in range(SHT):
                    act.wait_ge(s_shg, SHT * n + t + 1)
                    if n:
                        act.wait_ge(s_shhid, SHT * (n - 1) + t + 1)
                    act.activation(sgate[:, t, :], bank[t][:, :], ACT.Silu).then_inc(s_shsil, 1)
            for q in range(E * FT):
                e, j = divmod(q, FT)
                act.wait_ge(s_gu, q + 1)
                if q >= SGB:
                    act.wait_ge(s_hid, q - SGB + 1)
                act.activation(sgate_e[:, q % SGB, :], up_bank(q)[:, CAP:2 * CAP], ACT.Silu,
                               bias=biasT[:, 1, j, e:e + 1]).then_inc(s_sil, 1)
                if j == 2 and e > 0:
                    weigh(act, e - 1)
            weigh(act, E - 1)

        @block.vector
        def _(dve):
            step = [0]

            def link(ins):
                step[0] += 1
                ins.then_inc(s_dve, 1)
                dve.wait_ge(s_dve, step[0])

            def norm_stats(src, w):
                for i in range(w.start, w.stop):
                    last = dve.bn_stats(stats[:, i, :], src[:, i, 0:C])
                link(last)
                m_e, v_e, m_o, v_o = (stats[:, w, k] for k in (1, 2, 4, 5))
                dve.tensor_tensor(small[:, 1, w], m_e, m_o, ALU.subtract)
                dve.tensor_tensor(small[:, 2, w], v_e, v_o, ALU.add)
                link(dve.tensor_tensor(small[:, 0, w], m_e, m_o, ALU.add))
                link(dve.scalar_tensor_tensor(small[:, 3, w], small[:, 1, w], 0.25, small[:, 1, w], ALU.mult, ALU.mult))
                dve.scalar_tensor_tensor(small[:, 5, w], small[:, 2, w], 1.0 / C, small[:, 3, w],
                                         ALU.mult, ALU.add).then_inc(s_var, 1)

            def norm_apply(dst, src, w, sem_done, n):
                dve.wait_ge(s_rstd, n)
                link(dve.scalar_tensor_tensor(small[:, 4, w], small[:, 0, w], -0.5, small[:, 6, w], ALU.mult, ALU.mult))
                for i in range(w.start, w.stop):
                    last = dve.tensor_scalar(dst[:, i, 0:C], src[:, i, :], small[:, 6, i:i + 1], small[:, 4, i:i + 1],
                                             ALU.mult, ALU.add)
                    if i % 4 == 3:
                        last.then_inc(sem_done, 1)

            dve.wait_ge(s_ident, 1)
            dve.tensor_reduce(pick[:, :], ident[:, :].rearrange("p (a e) -> p e a", e=8), AX.X, ALU.add)
            for b in range(NB):
                dve.wait_ge(s_x[b], 16)
                norm_stats(x_tok, tiles(b))
            dve.wait_ge(s_const, 16)
            syn = taps[:, 8:16].rearrange("p (f k) -> p f k", f=2)
            dve.tensor_tensor(comb[:, :, 0:1], syn[:, :, 0:1], syn[:, :, 1:2], ALU.add)
            dve.tensor_tensor(comb[:, :, 1:2], syn[:, :, 2:3], syn[:, :, 3:4], ALU.add)
            link(dve.tensor_tensor(comb[:, :, 2:3], syn[:, :, 1:2], syn[:, :, 2:3], ALU.add))
            for k in range(4):
                dve.tensor_scalar(diag[:, k, :], ident[:, :], taps[:, 4 + k:5 + k], None, ALU.mult)
            for f in range(2):
                tap = [taps[:, 8 + 4 * f:9 + 4 * f], comb[:, f, 2:3], taps[:, 11 + 4 * f:12 + 4 * f],
                       comb[:, f, 0:1], comb[:, f, 1:2]]
                for k in range(5):
                    last = dve.tensor_scalar(diag[:, 4 + 5 * f + k, :], ident[:, :], tap[k], None, ALU.mult)
            last.then_inc(s_diag, 1)
            for b in range(NB):
                norm_apply(xn_tok, x_tok, tiles(b), s_xn, b + 1)
            for b in range(NB):
                dve.wait_ge(s_xp, 2 * b + 2)
                dst = l1p[:, b, 1:N1 + 1]
                link(dve.tensor_scalar(dst, xp[:, 1, b, 0:N1], taps[:, 0:1], None, ALU.mult))
                for k, (r, o) in ((1, (0, 1)), (2, (1, 1)), (3, (0, 2))):
                    ins = dve.scalar_tensor_tensor(dst, xp[:, r, b, o:o + N1], taps[:, k:k + 1], dst, ALU.mult, ALU.add)
                    if k < 3:
                        link(ins)
                ins.then_inc(s_l1, 1)
            dve.wait_ge(s_l1, NB)
            l2 = l2f[:, :].rearrange("p (b n) -> p b n", b=NB)
            link(dve.tensor_scalar(l2, l1p[:, :, 0:N1:2], taps[:, 0:1], None, ALU.mult))
            for k in range(1, 4):
                ins = dve.scalar_tensor_tensor(l2, l1p[:, :, k:k + N1:2], taps[:, k:k + 1], l2, ALU.mult, ALU.add)
                if k < 3:
                    link(ins)
            ins.then_inc(s_l2, 1)
            dve.wait_ge(s_l2, 1)
            link(dve.tensor_scalar(qf[:, :], l2f[:, :], 0.0, None, ALU.max))
            dve.wait_ge(s_exp, 1)
            dve.scalar_tensor_tensor(qf[:, :], expf[:, :], 1.0, qf[:, :], ALU.min, ALU.add).then_inc(s_q, 1)
            dve.wait_ge(s_q, 1)
            link(dve.tensor_reduce(zsum[:, :], qf[:, :].rearrange("p (b n) -> p b n", b=NB), AX.X, ALU.add))
            dve.wait_ge(s_qvT, 2)
            dve.tensor_copy(kT[:, :], bank[2][:, :]).then_inc(s_qve, 1)
            dve.wait_ge(s_masks, 1)
            for b in range(NB):
                dve.tensor_scalar(kvz[:, 1, b, :], same8[:, :], zsum[:, b:b + 1], None, ALU.mult)
            dve.wait_ge(s_kv, 1)
            dve.tensor_tensor(kvz[:, 0, :, :], bank[3][:, 0:256].rearrange("p (b n) -> p b n", b=NB),
                              same8[:, :].unsqueeze(1).to_broadcast([P, NB, P]), ALU.mult).then_inc(s_kvm, 1)
            dve.wait_ge(s_nd, 1)
            link(dve.tensor_scalar(den[:, :], bank[1][:, :], ATTN_EPS, None, ALU.add))
            link(dve.reciprocal(den[:, :], den[:, :]))
            dve.tensor_tensor(ap_[:, :, 1:N2 + 1], bank[2][:, :].rearrange("p (b n) -> p b n", b=NB),
                              den[:, :].rearrange("p (b n) -> p b n", b=NB), ALU.mult).then_inc(s_attn, 1)
            dve.wait_ge(s_up2, 1)
            dve.tensor_copy(r1p[:, :, 1:N1 + 1:2], bank[4][:, :].rearrange("p (b n) -> p b n", b=NB)).then_inc(s_r1, 1)
            for n in range(4):
                dve.wait_ge(s_up1, n + 1)
                link(dve.tensor_tensor(x1[:, 4 * n:4 * n + 4, :].rearrange("p i c -> p (i c)"), bank[n][:, :],
                                       xn_tok[:, 4 * n:4 * n + 4, :].rearrange("p i c -> p (i c)"), ALU.add))
            dve.wait_ge(s_xb, 1)
            for b in range(NB):
                norm_stats(x1, tiles(b))
            for b in range(NB):
                w = tiles(b)
                dve.wait_ge(s_rstd, 3 + b)
                link(dve.tensor_scalar(small[:, 4, w], small[:, 0, w], 0.5, None, ALU.mult))
                for i in range(w.start, w.stop):
                    last = dve.scalar_tensor_tensor(x1[:, i, :], x1[:, i, :], small[:, 4, i:i + 1], gamma_bc[:, :],
                                                    ALU.subtract, ALU.mult)
                link(last)
                for i in range(w.start, w.stop):
                    last = dve.scalar_tensor_tensor(x1[:, i, :], x1[:, i, :], small[:, 6, i:i + 1], x_tok[:, i, :],
                                                    ALU.mult, ALU.add)
                link(last)
                norm_stats(x1, w)
            for b in range(NB):
                norm_apply(hrow, x1, tiles(b), s_hn, 5 + b)
            dve.wait_ge(s_scT, 1)
            link(dve.tensor_copy(score2[:, :].rearrange("p (t r) -> p r t", r=2),
                                 bank[5][:, 0:256].rearrange("p (r t) -> p r t", r=2)))

            thr, cand, inc = ibits[:, 0:1], ibits[:, 1:2], ibits[:, 2:3]
            dve.memset(thr, 0)
            link(dve.memset(cand, 1 << (BITS - 1)))

            def shared_hid(n, t):
                dve.wait_ge(s_shsil, SHT * n + t + 1)
                dve.wait_ge(s_shu, SHT * n + t + 1)
                if n:
                    dve.wait_ge(s_shout, n)
                dve.tensor_tensor(sh_hid[:, t, :], bank[2 + t][:, :], sgate[:, t, :], ALU.mult).then_inc(s_shhid, 1)

            def shared_add(n):
                dve.wait_ge(s_shout, n + 1)
                dve.tensor_tensor(x1[:, 4 * n:4 * n + 4, :].rearrange("p i c -> p (i c)"), bank[4][:, :],
                                  x1[:, 4 * n:4 * n + 4, :].rearrange("p i c -> p (i c)"), ALU.add).then_inc(s_base, 1)

            for it in range(BITS):
                bit = BITS - 1 - it
                dve.tensor_scalar(junk[:, :], score2[:, :], cand.bitcast(F32), 0.0, ALU.is_ge, ALU.add,
                                  accum_out=cnt[:, 0:1]).then_inc(s_cnt, 1)
                fill(it, {4: lambda n: shared_hid(n, 0), 6: lambda n: shared_hid(n, 1), 11: shared_add})
                dve.wait_ge(s_tot, it + 1)
                link(dve.tensor_scalar(inc, bank[5][:, 511:512], float(CAP), float(1 << bit), ALU.is_ge, ALU.mult))
                if bit:
                    dve.scalar_tensor_tensor(cand, inc, 1 << (bit - 1), thr, ALU.bitwise_or, ALU.bitwise_or)
                link(dve.tensor_tensor(thr, thr, inc, ALU.bitwise_or))

            gt, eq, scan, chosen, pos = (sel[:, k, :] for k in range(5))
            thr_f = thr.bitcast(F32)
            dve.tensor_scalar(gt, score2[:, :], thr_f, 0.0, ALU.is_gt, ALU.add, accum_out=cnt[:, 1:2])
            dve.tensor_scalar(eq, score2[:, :], thr_f, 0.0, ALU.is_equal, ALU.add,
                              accum_out=cnt[:, 2:3]).then_inc(s_cnt, 1)
            dve.wait_ge(s_cnt, BITS + 1)
            link(dve.tensor_tensor_scan(scan, eq, eq, 0.0, ALU.add, ALU.max))
            dve.wait_ge(s_tot, BITS + 1)
            link(dve.tensor_scalar(rneed[:, :], bank[5][:, 511:512], -1.0, float(CAP), ALU.mult, ALU.add))
            link(dve.scalar_tensor_tensor(eq, scan, rneed[:, :], eq, ALU.is_le, ALU.mult))
            dve.scalar_tensor_tensor(chosen, eq, 1.0, gt, ALU.mult, ALU.add, accum_out=cnt[:, 3:4]).then_inc(s_cnt, 1)
            dve.wait_ge(s_cnt, BITS + 2)
            link(dve.tensor_tensor_scan(scan, chosen, chosen, 0.0, ALU.add, ALU.max))
            dve.wait_ge(s_tot, BITS + 2)
            dve.scalar_tensor_tensor(pos, scan, bank[5][:, 511:512], chosen, ALU.add, ALU.mult).then_inc(s_pos, 1)
            dve.wait_ge(s_posT, 1)
            link(dve.tensor_scalar(slot_i[:, 0, :].rearrange("p (r k e) -> p r k e", r=2, k=BLK),
                                   bank[5][:, 0:256].rearrange("p (r e k) -> p r k e", r=2, k=BLK),
                                   -1.0, None, ALU.add))
            dve.tensor_scalar(slot_i[:, 1, :], slot_i[:, 0, :], 4, None, ALU.arith_shift_right)
            link(dve.tensor_scalar(slot_i[:, 2, :], slot_i[:, 0, :], HI - 1, None, ALU.bitwise_and))
            link(dve.tensor_copy(slot_h[:, :, :], slot_i[:, 1:3, :]))
            for a in range(HI):
                dve.tensor_scalar(one_hi[:, :, a, :], slot_h[:, 0, :].rearrange("p (n e) -> p n e", e=8), float(a), None, ALU.is_equal)
            for a in range(HI):
                last = dve.tensor_scalar(one_lo[:, :, a, :], slot_h[:, 1, :].rearrange("p (n e) -> p n e", e=8), float(a), None, ALU.is_equal)
            link(last)
            dve.tensor_tensor(one_lo[:, :, :, :], one_lo[:, :, :, :],
                              token_no[:, :].rearrange("p (n e) -> p n e", e=8).unsqueeze(2).to_broadcast([P, 32, HI, 8]),
                              ALU.mult).then_inc(s_hot, 1)
            dve.wait_ge(s_tab, 1)
            link(dve.tensor_tensor(ext[:, :].rearrange("p (b e) -> p b e", e=8),
                                   bank[5][:, 0:256].rearrange("p (b e) -> p b e", e=8),
                                   pick[:, :].unsqueeze(1).to_broadcast([P, 32, 8]), ALU.mult))
            dve.tensor_reduce(itab[:, :], ext[:, :].rearrange("p (b e) -> p b e", e=8), AX.X, ALU.add).then_inc(s_itab, 1)
            dve.wait_ge(s_itT, 1)
            dve.tensor_copy(itabT[:, :], bank[5][0:HI, 0:256]).then_inc(s_itTe, 1)
            dve.wait_ge(s_spread, 1)
            link(dve.tensor_tensor(ext[:, :].rearrange("p (g e a) -> p g e a", g=4, e=8),
                                   bank[5][:, 256:512].rearrange("p (g a e) -> p g e a", g=4, e=8),
                                   pick[:, :].unsqueeze(1).unsqueeze(1).to_broadcast([P, 4, 8, 8]), ALU.mult))
            dve.tensor_reduce(rows[:, :, :, :].rearrange("p g c e -> p (g c e)"),
                              ext[:, :].rearrange("p (m a) -> p m a", a=8), AX.X, ALU.add).then_inc(s_rows, 1)

            def keep_x(e):
                dve.wait_ge(s_xsT, e + 1)
                if e >= 2:
                    dve.wait_ge(s_gu, FT * (e - 1))
                dve.tensor_copy(xselT[:, e % 2, :], bank[5][:, 0:CAP]).then_inc(s_xs, 1)

            def add_bias(e):
                dve.wait_ge(s_dn, e + 1)
                if e >= 2:
                    dve.wait_ge(s_scat, 16 * CH * (e - 1))
                dve.tensor_tensor(eo[:, e % 2, :, :], bank[3 + e % 2][:, 0:CAP].rearrange("p (c d) -> p c d", c=CH),
                                  down_b_bc[:, e, :].unsqueeze(1).to_broadcast([P, CH, C]), ALU.add).then_inc(s_eb, 1)

            dve.wait_ge(s_db_in, 16)
            keep_x(0)
            for q in range(E * FT):
                e, j = divmod(q, FT)
                dve.wait_ge(s_sil, q + 1)
                if e >= 2:
                    dve.wait_ge(s_dn, e - 1)
                dve.scalar_tensor_tensor(hidden[:, e % 2, j, :], up_bank(q)[:, 0:CAP], biasT[:, 0, j, e:e + 1],
                                         sgate_e[:, q % SGB, :], ALU.add, ALU.mult).then_inc(s_hid, 1)
                if j == 1 and e > 0:
                    add_bias(e - 1)
                if j == 2 and e + 1 < E:
                    keep_x(e + 1)
            add_bias(E - 1)

        @block.tensor
        def _(pe):
            pe.wait_ge(s_ident, 1)
            for b in range(NB):
                for r in range(2):
                    pe.wait_ge(s_xn, 2 * b + 2)
                    for k in range(BPB):
                        last = pe.transpose(bank[2 * b + r][:, k * P:(k + 1) * P], xn_tok[:, 2 * (b * BPB + k) + r, :],
                                            ident[:, :])
                    last.then_inc(s_xnT, 1)
            pe.wait_ge(s_diag, 1)
            for b in range(NB):
                pe.wait_ge(s_xp, 4)
                for k, (r, o) in enumerate(((1, 0), (0, 1), (1, 1), (0, 2))):
                    last = pe.matmul(bank[b][:, :], diag[:, k, :], xp[:, r, b, o:o + N1], start=(k == 0), stop=(k == 3))
                last.then_inc(s_h1, 1)
            pe.wait_ge(s_l1, NB)
            pe.wait_ge(s_h1e, 1)
            for k in range(4):
                last = pe.matmul(bank[0][:, :], diag[:, k, :], l1p[:, :, k:k + N1:2], start=(k == 0), stop=(k == 3))
            last.then_inc(s_h2, 1)
            pe.wait_ge(s_l2, 1)
            pe.wait_ge(s_h1e, 2)
            for k in range(4):
                last = pe.transpose(bank[1][:, k * P:(k + 1) * P], l2f[:, k * P:(k + 1) * P], ident[:, :])
            last.then_inc(s_qvT, 1)
            pe.wait_ge(s_q, 1)
            for k in range(4):
                last = pe.transpose(bank[2][:, k * P:(k + 1) * P], qf[:, k * P:(k + 1) * P], ident[:, :])
            last.then_inc(s_qvT, 1)
            pe.wait_ge(s_h2e, 1)
            TAPS = ((0, ((0, 0), (1, 1), (2, 2))), (1, ((3, 1), (4, 2))))
            for par, taps_of in TAPS:
                for k, o in taps_of:
                    pe.matmul(bank[4 + par][:, :], diag[:, 9 + k, :], h2p[:, :, o:o + N2], start=(k in (0, 3)), stop=False,
                              skip_group_check=True)
            pe.wait_ge(s_qve, 2)
            for b in range(NB):
                for k in range(2):
                    o = (2 * b + k) * P
                    last = pe.matmul(bank[3][:, b * P:(b + 1) * P], kT[:, o:o + P], vT[:, o:o + P],
                                     start=(k == 0), stop=(k == 1))
            last.then_inc(s_kv, 1)
            pe.wait_ge(s_kvm, 1)
            for b in range(NB):
                o = slice(b * N2, (b + 1) * N2)
                pe.matmul(bank[1][:, o], kvz[:, 1, b, :], qf[:, o], start=True, stop=True)
                last = pe.matmul(bank[2][:, o], kvz[:, 0, b, :], qf[:, o], start=True, stop=True)
            last.then_inc(s_nd, 1)
            pe.wait_ge(s_attn, 1)
            for par, taps_of in TAPS:
                for k, o in taps_of:
                    last = pe.matmul(bank[4 + par][:, :], diag[:, 4 + k, :], ap_[:, :, o:o + N2], start=False,
                                     stop=(o == 2), skip_group_check=True)
            last.then_inc(s_up2, 1)
            def synth(n, band, d0, begin):
                for t in range(4):
                    i = 4 * n + t
                    blk, par = divmod(i, 2)
                    b, m0 = blk // BPB, (blk % BPB) * P
                    for k, o in TAPS[par][1]:
                        last = pe.matmul(bank[n][:, t * P:(t + 1) * P], band[:, b, m0 + o:m0 + o + P], diag[:, d0 + k, :],
                                         start=(begin and t == 0 and k == 0), stop=(not begin and o == 2),
                                         skip_group_check=True)
                return last

            for n in range(4):
                synth(n, h1p, 9, True)
            pe.wait_ge(s_r1, 2)
            for n in range(4):
                synth(n, r1p, 4, False).then_inc(s_up1, 1)
            for n in range(4):
                pe.wait_ge(s_hn, n + 1)
                for t in range(4):
                    last = pe.transpose(bank[n][:, t * P:(t + 1) * P], hrow[:, 4 * n + t, 0:C], ident[:, :])
                last.then_inc(s_hTp, 1)
            pe.wait_ge(s_r1, 2)
            pe.wait_ge(s_const, 16)
            for i in range(NT):
                pe.wait_ge(s_hT, i // 4 + 1)
                blk, par = divmod(i, 2)
                o = par * P + blk
                last = pe.matmul(bank[4][:, o:par * P + P:BLK], hT[:, i, :], gate_wT, start=True, stop=True)
            last.then_inc(s_logit, 1)
            pe.wait_ge(s_score, 1)
            for r in range(2):
                last = pe.transpose(bank[5][:, r * P:(r + 1) * P], sel[:, 0, r * P:(r + 1) * P], ident[:, :])
            last.then_inc(s_scT, 1)
            pe.wait_ge(s_masks, 1)

            def count(n, *pairs):
                pe.wait_ge(s_cnt, n)
                for k, (mask, col) in enumerate(pairs):
                    last = pe.matmul(bank[5][:, 511:512], mask[:, :], cnt[:, col:col + 1], start=(k == 0),
                                     stop=(k == len(pairs) - 1))
                last.then_inc(s_tot, 1)

            def shared_up(n, t, kind):
                if n:
                    pe.wait_ge(s_shhid, SHT * (n - 1) + t + 1)
                rhs = hT[:, 4 * n:4 * n + 4, :].rearrange("p i t -> p (i t)")
                pe.matmul(bank[2 * kind + t][:, :], sh_wT[:, 2 * kind + t, :], rhs, start=True,
                          stop=True).then_inc((s_shg, s_shu)[kind], 1)

            def shared_down(n, half):
                if half == 0:
                    pe.wait_ge(s_shhid, SHT * (n + 1))
                    if n:
                        pe.wait_ge(s_base, n)
                for t in (2 * half, 2 * half + 1):
                    for k in range(SHT):
                        last = pe.matmul(bank[4][:, t * P:(t + 1) * P], sh_hid[:, k, t * P:(t + 1) * P], sh_wT[:, 4 + k, :],
                                         start=(k == 0), stop=(k == SHT - 1))
                if half:
                    last.then_inc(s_shout, 1)

            pe.wait_ge(s_shw, 16)
            pe.wait_ge(s_scT, 1)
            for it in range(BITS):
                count(it + 1, (same8_bf, 0))
                fill(it, {0: lambda n: shared_up(n, 0, 0), 1: lambda n: shared_up(n, 0, 1),
                          4: lambda n: shared_up(n, 1, 0), 5: lambda n: shared_up(n, 1, 1),
                          8: lambda n: shared_down(n, 0), 9: lambda n: shared_down(n, 1)})
            count(BITS + 1, (same8_bf, 1), (earlier, 2))
            count(BITS + 2, (earlier, 3))
            pe.wait_ge(s_pos, 1)
            for r in range(2):
                last = pe.transpose(bank[5][:, r * P:(r + 1) * P], sel[:, 4, r:256:2], ident[:, :])
            last.then_inc(s_posT, 1)
            pe.wait_ge(s_hot, 1)
            for g in range(2):
                for i in range(NT):
                    n = 2 * i + g
                    last = pe.matmul(bank[5][:, g * P:(g + 1) * P], one_hi[:, n, :, :].rearrange("p a e -> p (a e)"),
                                     one_lo[:, n, :, :].rearrange("p b e -> p (b e)"), start=(i == 0), stop=(i == NT - 1))
            last.then_inc(s_tab, 1)
            pe.wait_ge(s_itab, 1)
            for g in range(2):
                last = pe.transpose(bank[5][0:HI, g * P:(g + 1) * P], itab[:, g * HI:(g + 1) * HI], ident[:, :])
            last.then_inc(s_itT, 1)
            pe.wait_ge(s_itTe, 1)
            pe.matmul(bank[5][:, 256:512], sel_lo[:, :], itabT[:, :], start=True, stop=True).then_inc(s_spread, 1)

            def turn_x(e):
                pe.wait_ge(s_gath[e % GBUF], 16 * CH * (e // GBUF + 1))
                if e == 0:
                    pe.wait_ge(s_rows, 1)
                else:
                    pe.wait_ge(s_xs, e)
                for c in range(CH):
                    last = pe.transpose(bank[5][:, c * P:(c + 1) * P], gath[:, e % GBUF, c, 0:C], ident[:, :])
                last.then_inc(s_xsT, 1)

            LAG = 3

            def down(q):
                e, j = divmod(q, FT)
                pe.wait_ge(s_hid, q + 1)
                if j == 0 and e >= 2:
                    pe.wait_ge(s_eb, e - 1)
                for c in range(CH):
                    last = pe.matmul(bank[3 + e % 2][:, c * P:(c + 1) * P], hidden[:, e % 2, j, c * P:(c + 1) * P],
                                     wT[:, e, 2, j, :], start=(j == 0 and c == 0), stop=(j == FT - 1),
                                     skip_group_check=True)
                if j == FT - 1:
                    last.then_inc(s_dn, 1)

            pe.wait_ge(s_base, 4)
            turn_x(0)
            for q in range(E * FT):
                e, j = divmod(q, FT)
                if j == 0:
                    pe.wait_ge(s_wT[e], 16)
                    pe.wait_ge(s_xs, e + 1)
                if q >= len(UP_BANKS):
                    pe.wait_ge(s_hid, q - len(UP_BANKS) + 1)
                pe.matmul(up_bank(q)[:, 0:CAP], wT[:, e, 0, j, :], xselT[:, e % 2, :], start=True, stop=True)
                pe.matmul(up_bank(q)[:, CAP:2 * CAP], wT[:, e, 1, j, :], xselT[:, e % 2, :], start=True,
                          stop=True).then_inc(s_gu, 1)
                if q >= LAG:
                    down(q - LAG)
                if j == 1 and e + 1 < E:
                    turn_x(e + 1)
            for q in range(E * FT - LAG, E * FT):
                down(q)


_OUTS = [((2, 1024, 128), 'float32')]


def _laid_out(inputs):
    import numpy as np
    v = {k: np.asarray(a) for k, a in inputs.items()}
    attn = lambda n: v["L0_attn_" + n]
    ffn = lambda n: v["L0_ffn_" + n]
    E, F, D = ffn("up_w").shape
    ft, sh = F // 128, ffn("sh_up_w").shape[0] // 128
    bias = [b.reshape(E, ft, 128).transpose(2, 1, 0).reshape(128, ft * E) for b in (ffn("up_b"), ffn("gb"))]
    packed = np.concatenate([attn(n).T for n in ("h_filter", "g_filter", "h_synth", "g_synth")]
                            + [ffn("gate_w").T] + bias
                            + [np.broadcast_to(attn(n), (128, D)) for n in ("norm_gamma", "norm_beta")], axis=1)
    rise = [w.reshape(E, ft, 128, D).transpose(0, 3, 1, 2) for w in (ffn("up_w"), ffn("gw"))]
    fall = ffn("down_w").reshape(E, D, ft, 128).transpose(0, 3, 2, 1)
    weights = np.stack(rise + [fall], axis=2)
    s_rise = [w.reshape(sh, 128, D).transpose(2, 0, 1) for w in (ffn("sh_gate_w"), ffn("sh_up_w"))]
    s_fall = ffn("sh_down_w").reshape(D, sh, 128).transpose(2, 1, 0)
    shared = np.concatenate(s_rise + [s_fall], axis=1)
    return {n: np.ascontiguousarray(a) for n, a in (("x", attn("x")), ("packed", packed), ("weights", weights),
                                                    ("shared", shared), ("down_b", ffn("down_b")))}


def kernel(**inputs):
    import numpy as _np
    import concourse.bacc as _bacc
    from concourse import mybir as _mybir
    from concourse.bass_utils import run_bass_kernel_spmd as _run

    nc = _bacc.Bacc("TRN2", target_bir_lowering=False, num_devices=1)
    arrays, args = {}, []
    for name, a in _laid_out(inputs).items():
        arrays[f"in_{name}_dram"] = a
        args.append(nc.dram_tensor(f"in_{name}_dram", a.shape, _mybir.dt.from_np(a.dtype), kind="ExternalInput").ap())
    for i, (shape, dtype) in enumerate(_OUTS):
        dt = _mybir.dt.from_np(_np.dtype(dtype))
        args.append(nc.dram_tensor(f"out_{i}_dram", shape, dt, kind="ExternalOutput").ap())
    wavelet_attention_moe(nc, *args)
    r = _run(nc, [arrays], core_ids=[0])
    return r.results[0]["out_0_dram"]
```

```python
from contextlib import ExitStack

import concourse.bass as bass
from concourse import mybir

ALU = mybir.AluOpType
ACT = mybir.ActivationFunctionType
AX = mybir.AxisListType
F32 = mybir.dt.float32
F16 = mybir.dt.float16
BF16 = mybir.dt.bfloat16
I32 = mybir.dt.int32
U32 = mybir.dt.uint32
U16 = mybir.dt.uint16

P = 128
LN_EPS = 1e-5
ATTN_EPS = 1e-6
HEAD = 8


def wavelet_attention_moe(nc, x, packed, weights, shared, down_b, out):
    NB, SEQ, C = x.shape
    TOK = NB * SEQ
    E, _, KINDS, FT, _ = weights.shape
    SHT = shared.shape[1] // KINDS
    CAP = -(-TOK * 2 // E)
    BLK = TOK // 256
    BPB = BLK // NB
    NT = TOK // P
    N1, N2 = SEQ // 2, SEQ // 4
    ROW = C + E
    GBUF = 6
    CH = CAP // P
    BITS = 30
    LOW = 14
    HI = 16

    h_rows = nc.dram_tensor("h_rows", [TOK, ROW], F32)

    ctx = ExitStack()
    with ctx:
        ctx.enter_context(nc.allow_low_precision(reason="exact integers"))

        def sb(name, shape, dt=F32):
            return ctx.enter_context(nc.sbuf_tensor(name, shape, dt))

        def sem(name):
            return ctx.enter_context(nc.semaphore(name))

        bank = [ctx.enter_context(nc.psum_tensor(f"bank{i}", [P, 512], F32)) for i in range(8)]

        ident = sb("ident", [P, P])
        same8 = sb("same8", [P, P])
        same8_bf = sb("same8_bf", [P, P], BF16)
        earlier = sb("earlier", [P, P], BF16)
        pick = sb("pick", [P, 8])
        sel_lo = sb("sel_lo", [HI, P])
        token_no = sb("token_no", [P, 2 * P], F16)
        half_pow = sb("half_pow", [P, NT])
        consts = sb("consts", [P, packed.shape[1]])
        taps = consts[:, 0:16]
        gate_wT = consts[:, 16:32]
        biasT = consts[:, 32:160].rearrange("p (k j e) -> p k j e", k=2, j=FT)
        gamma_bc = consts[:, 160:160 + C]
        beta_bc = consts[:, 160 + C:160 + 2 * C]
        kvz = sb("kvz", [P, NB, C + C // HEAD])
        rden = sb("rden", [P, NB, N2 // P, C // HEAD])
        attn_tok = sb("attn_tok", [P, NB, N2 // P, C])
        comb = sb("comb", [P, 2, 3])
        diag = sb("diag", [P, 14, P])
        sh_wT = sb("sh_wT", [P, 6, P])

        x_tok = sb("x_tok", [P, NT, C])
        x1 = sb("x1", [P, NT, C])
        hrow = sb("hrow", [P, NT, ROW])
        hT = sb("hT", [P, NT, P])
        wT = sb("wT", [P, E, KINDS, FT, P])

        area = sb("area", [P, 2048 + 4 * 514 + 2 * 516 + 2 * 514 * 2 + 4 * 258])
        at = [0]

        def carve(n, base=None):
            if base is not None:
                at[0] = base
            a = area[:, at[0]:at[0] + n]
            at[0] += n
            return a

        xn_tok = carve(2048, 0).rearrange("p (i c) -> p i c", i=NT)
        xp = carve(4 * 514).rearrange("p (r b n) -> p r b n", r=2, b=NB)
        l1p = carve(2 * 516).rearrange("p (b n) -> p b n", b=NB)
        h1p = carve(2 * 514).rearrange("p (b n) -> p b n", b=NB)
        r1p = carve(2 * 514).rearrange("p (b n) -> p b n", b=NB)
        h2p = carve(2 * 258).rearrange("p (b n) -> p b n", b=NB)
        ap_ = carve(2 * 258).rearrange("p (b n) -> p b n", b=NB)
        one_hi = carve(2048, 0).bitcast(F16).rearrange("p (n a e) -> p n a e", a=HI, e=8)
        one_lo = carve(2048).bitcast(F16).rearrange("p (n b e) -> p n b e", b=HI, e=8)
        sel = carve(5 * 256).rearrange("p (k n) -> p k n", k=5)
        key = carve(3 * 128).bitcast(U16).rearrange("p (k n) -> p k n", k=3)
        bits = carve(512).bitcast(I32).rearrange("p (k n) -> p k n", k=2)
        carve(128)
        slot_i = carve(3 * 256).bitcast(I32).rearrange("p (k n) -> p k n", k=3)
        slot_h = carve(256).bitcast(F16).rearrange("p (k n) -> p k n", k=2)
        ext = carve(256)
        score2 = carve(256)
        xselT = carve(2 * CAP, 4104).rearrange("p (s n) -> p s n", s=2)
        hidden = carve(2 * FT * CAP).rearrange("p (s j n) -> p s j n", s=2, j=FT)
        eo = carve(2 * CH * C).rearrange("p (s c d) -> p s c d", s=2, c=CH)
        flat_hT = hT[:, :, :].rearrange("p i t -> p (i t)")
        flat_hrow = hrow[:, :, :].rearrange("p i t -> p (i t)")
        gath = flat_hT[:, 0:GBUF * CH * ROW].rearrange("p (s c r) -> p s c r", s=GBUF, c=CH)
        l2f, expf, qf, vT = (flat_hT[:, 512 * k:512 * k + 512] for k in range(4))
        kT = flat_hrow[:, 0:512]
        down_b_bc = x_tok
        junk = sb("junk", [P, 3, 256], BF16)
        sgate = sb("sgate", [P, 2, 512])
        SGB = 1024 // CAP
        sgate_e = sgate[:, :, :].rearrange("p t n -> p (t n)").rearrange("p (s n) -> p s n", n=CAP)
        UP_BANKS = [bank[i] for i in (0, 1, 2, 6, 7)]

        def up_bank(q):
            return UP_BANKS[q % len(UP_BANKS)]

        stats = sb("stats", [P, NT, 6])
        mean_var = sb("mean_var", [P, NT, 2])
        var_eps = sb("var_eps", [P, NT])
        rstd = sb("rstd", [P, NT])
        shift = sb("shift", [P, NT])
        zsum = sb("zsum", [P, 2])
        cnt = sb("cnt", [P, 4], BF16)
        search = sb("search", [P, 16])
        sh_hid = sb("sh_hid", [P, 2, 2, 512])
        sh_up = sb("sh_up", [P, 2, 512])
        sh_down = sb("sh_down", [P, 512])
        itab = sb("itab", [P, 32])
        itabT = sb("itabT", [HI, 256])
        rows = sb("rows", [P, 2, CH, 8], U32)

        s_x = [sem(f"s_x{b}") for b in range(NB)]
        s_db_in = sem("s_db_in")
        s_wT = [sem(f"s_wT{e}") for e in range(E)]
        s_shw = sem("s_shw")
        s_ident = sem("s_ident")
        s_pool = sem("s_pool")
        s_masks = sem("s_masks")
        s_diag = sem("s_diag")
        s_comb = sem("s_comb")
        s_xb = sem("s_xb")
        s_rstd = sem("s_rstd")
        s_const = sem("s_const")
        s_shift = sem("s_shift")
        s_pad = sem("s_pad")
        s_xnv = sem("s_xnv")
        s_xna = sem("s_xna")
        s_h1 = sem("s_h1")
        s_h1a = sem("s_h1a")
        s_h1p = sem("s_h1p")
        s_h2 = sem("s_h2")
        s_vT = sem("s_vT")
        s_kT = sem("s_kT")
        s_attn = sem("s_attn")
        s_attnT = sem("s_attnT")
        s_apv = sem("s_apv")
        s_apa = sem("s_apa")
        s_up2h = sem("s_up2h")
        s_up2 = sem("s_up2")
        s_r1v = sem("s_r1v")
        s_r1a = sem("s_r1a")
        s_stats = sem("s_stats")
        s_aff = sem("s_aff")
        s_x1b = sem("s_x1b")
        s_hnv = sem("s_hnv")
        s_hna = sem("s_hna")
        s_xnT = sem("s_xnT")
        s_xp = sem("s_xp")
        s_l1 = sem("s_l1")
        s_l2 = sem("s_l2")
        s_exp = sem("s_exp")
        s_q = sem("s_q")
        s_qvT = sem("s_qvT")
        s_kv = sem("s_kv")
        s_kvm = sem("s_kvm")
        s_nd = sem("s_nd")
        s_up1 = sem("s_up1")
        s_hTp = sem("s_hTp")
        s_hT = sem("s_hT")
        s_logit = sem("s_logit")
        s_score = sem("s_score")
        s_scT = sem("s_scT")
        s_hrow = sem("s_hrow")
        s_hstore = sem("s_hstore")
        s_cnt = sem("s_cnt")
        s_tot = sem("s_tot")
        s_shg = sem("s_shg")
        s_shu = sem("s_shu")
        s_shdn = sem("s_shdn")
        s_shupe = sem("s_shupe")
        s_shsil = sem("s_shsil")
        s_shhid = sem("s_shhid")
        s_shout = sem("s_shout")
        s_base = sem("s_base")
        s_store = sem("s_store")
        s_pos = sem("s_pos")
        s_posT = sem("s_posT")
        s_hot = sem("s_hot")
        s_tab = sem("s_tab")
        s_itab = sem("s_itab")
        s_itT = sem("s_itT")
        s_itTe = sem("s_itTe")
        s_spread = sem("s_spread")
        s_rows = sem("s_rows")
        s_gath = [sem(f"s_gath{i}") for i in range(GBUF)]
        s_xsT = sem("s_xsT")
        s_xs = sem("s_xs")
        s_gu = sem("s_gu")
        s_sil = sem("s_sil")
        s_hid = sem("s_hid")
        s_dn = sem("s_dn")
        s_eb = sem("s_eb")
        s_eo = sem("s_eo")
        s_scat = sem("s_scat")
        s_dve = sem("s_dve")

        x_v = x.rearrange("b (k p r) c -> p (b k) (r c)", p=P, r=2)
        out_v = out.rearrange("b (k p r) c -> p (b k) (r c)", p=P, r=2)
        out_rows = out.rearrange("b s c -> (b s) c")
        h_v = h_rows[:, :].rearrange("(k p r) c -> p k (r c)", p=P, r=2)

        PHASE = ((1, 0), (0, 1), (1, 1), (0, 2))
        TAPS = (((0, 0), (1, 1), (2, 2)), ((3, 1), (4, 2)))

        def tap_sum(f, k):
            return (taps[:, 8 + 4 * f:9 + 4 * f], comb[:, f, 2:3], taps[:, 11 + 4 * f:12 + 4 * f],
                    comb[:, f, 0:1], comb[:, f, 1:2])[k]

        NORMS = [("x", 0), ("x", 1), ("t", 0), ("t", 1), ("x1", 0), ("t", 2), ("x1", 1), ("t", 3), ("x1", 2), ("x1", 3)]

        def norm_no(kind, g):
            return NORMS.index((kind, g)) + 1

        def norm_tiles_of(n):
            kind, g = NORMS[n - 1]
            return tiles(g) if kind == "x" else group(g)

        LAST = NT // 4 - 1

        def group(g):
            return slice(4 * g, 4 * g + 4)

        def psum_t(i):
            return bank[i // 4][:, (i % 4) * P:(i % 4 + 1) * P]

        def tiles(b):
            return slice(b * NT // NB, (b + 1) * NT // NB)

        ROUNDS = [b for b in range(BITS - LOW - 2, -1, -2)] + [b for b in range(LOW - 2, -1, -2)]
        PERIOD = 5

        block = ctx.enter_context(nc.Block())

        @block.sync
        def _(sp):
            def load_x(b):
                sp.dma_start(x_tok[:, tiles(b), :].rearrange("p (k r) c -> p k (r c)", r=2),
                             x_v[:, b * BPB:(b + 1) * BPB, :]).then_inc(s_x[b], 16)

            load_x(0)
            sp.dma_start(consts[:, :], packed).then_inc(s_const, 16)
            load_x(1)
            sp.dma_start(sh_wT[:, :, :], shared).then_inc(s_shw, 16)
            for e in range(E):
                sp.dma_start(wT[:, e, :, :, :], weights[e]).then_inc(s_wT[e], 16)
            for b in range(NB):
                sp.wait_ge(s_hna, 2 * (b + 1))
                if b == NB - 1:
                    sp.wait_ge(s_hnv, 1)
                sp.wait_ge(s_hrow, 1)
                sp.dma_start(h_v[:, b * BPB:(b + 1) * BPB, :],
                             hrow[:, tiles(b), :].rearrange("p (k r) c -> p k (r c)", r=2)).then_inc(s_hstore, 16)
            sp.dma_start(down_b_bc[:, :, :].rearrange("p e c -> p (e c)"),
                         down_b.rearrange("e c -> (e c)").partition_broadcast(P)).then_inc(s_db_in, 16)
            for n in range(NT // 4):
                sp.wait_ge(s_base, n + 1)
                sp.dma_start(out_v[:, 2 * n:2 * n + 2, :],
                             x1[:, 4 * n:4 * n + 4, :].rearrange("p (k r) c -> p k (r c)", r=2)).then_inc(s_store, 16)
            sp.wait_ge(s_hstore, 16 * NB)
            sp.wait_ge(s_store, 16 * (NT // 4))
            sp.wait_ge(s_scat, 16 * CH * E)

        @block.gpsimd
        def _(pool):
            step = [0]

            def link(ins):
                step[0] += 1
                ins.then_inc(s_pool, 1)
                pool.wait_ge(s_pool, step[0])

            link(pool.memset(ident[:, :], 0.0))
            pool.affine_select(out=ident[:, :], in_=ident[:, :], compare_op=ALU.not_equal, fill=1.0, base=0,
                               pattern=[[-1, P]], channel_multiplier=1).then_inc(s_ident, 1)
            pool.memset(half_pow[:, :], -0.5)
            pool.memset(xp[:, :, :, 0:1], 0.0)
            pool.memset(xp[:, :, :, N1 + 1:N1 + 2], 0.0)
            pool.memset(l1p[:, :, 0:1], 0.0)
            pool.memset(l1p[:, :, N1 + 1:N1 + 4], 0.0)
            for band, n in ((h1p, N1), (r1p, N1), (h2p, N2), (ap_, N2)):
                pool.memset(band[:, :, 0:1], 0.0)
                last = pool.memset(band[:, :, n + 1:n + 2], 0.0)
            last.then_inc(s_pad, 1)
            link(pool.memset(same8[:, :], 1.0))
            link(pool.affine_select(out=same8[:, :], in_=same8[:, :], compare_op=ALU.is_ge, fill=0.0, base=0,
                                    pattern=[[-8, 16], [0, 8]], channel_multiplier=1))
            link(pool.affine_select(out=same8[:, :], in_=same8[:, :], compare_op=ALU.is_ge, fill=0.0, base=7,
                                    pattern=[[8, 16], [0, 8]], channel_multiplier=-1))
            pool.tensor_copy(same8_bf[:, :], same8[:, :])
            pool.affine_select(out=earlier[:, :], in_=same8[:, :], compare_op=ALU.is_ge, fill=0.0, base=-1,
                               pattern=[[1, P]], channel_multiplier=-1)
            link(pool.memset(sel_lo[:, :], 1.0))
            link(pool.affine_select(out=sel_lo[:, :], in_=sel_lo[:, :], compare_op=ALU.is_ge, fill=0.0, base=0,
                                    pattern=[[1, P]], channel_multiplier=-8))
            link(pool.affine_select(out=sel_lo[:, :], in_=sel_lo[:, :], compare_op=ALU.is_ge, fill=0.0, base=7,
                                    pattern=[[-1, P]], channel_multiplier=8))
            pool.iota(token_no[:, :], pattern=[[1, 2], [256, BLK], [0, E]], base=0, channel_multiplier=2,
                      allow_small_or_imprecise_dtypes=True).then_inc(s_masks, 1)

            def norm_scale(n):
                w = norm_tiles_of(n)
                pool.wait_ge(s_stats, n)
                pool.tensor_tensor(rstd[:, w], var_eps[:, w], half_pow[:, w], ALU.pow).then_inc(s_rstd, 1)

            norm_scale(1)
            norm_scale(2)
            pool.wait_ge(s_const, 16)
            pool.wait_ge(s_xp, 4)
            acc, part = h1p[:, 1, 1:N1 + 1], sgate[:, 0, :]
            for k, (r, o) in enumerate(PHASE):
                dst = part if k else acc
                link(pool.tensor_tensor(dst, xp[:, r, 1, o:o + N1], taps[:, 4 + k:5 + k].to_broadcast([P, N1]), ALU.mult))
                if k:
                    ins = pool.tensor_tensor(acc, acc, part, ALU.add)
                    if k < 3:
                        link(ins)
            ins.then_inc(s_h1p, 1)
            pool.wait_ge(s_xnv, NB)
            pool.wait_ge(s_xna, NB)
            pool.tensor_tensor(x_tok[:, :, :], x_tok[:, :, :],
                               beta_bc.unsqueeze(1).to_broadcast([P, NT, C]), ALU.add).then_inc(s_xb, 1)
            for n in range(3, len(NORMS) + 1):
                norm_scale(n)

            def shared_add(n):
                pool.wait_ge(s_shdn, n + 1)
                x1_n = x1[:, group(n), :].rearrange("p i c -> p (i c)")
                pool.tensor_tensor(x1_n, sh_down[:, :], x1_n, ALU.add).then_inc(s_base, 1)

            pool.wait_ge(s_hna, LAST + 1)
            pool.wait_ge(s_hnv, 1)
            for n in range(LAST + 1):
                for t in range(SHT):
                    pool.wait_ge(s_shsil, SHT * n + t + 1)
                    pool.wait_ge(s_shupe, SHT * n + t + 1)
                    if n >= 2:
                        pool.wait_ge(s_shout, n - 1)
                    pool.tensor_tensor(sh_hid[:, n % 2, t, :], sh_up[:, t, :], sgate[:, t, :], ALU.mult).then_inc(s_shhid, 1)
                if n:
                    shared_add(n - 1)

            def gather(e):
                g, k = divmod(e, 8)
                if e % 8 == 0:
                    pool.wait_ge(s_rows, g + 1)
                if e >= GBUF:
                    pool.wait_ge(s_eo, CH * (e - GBUF + 1))
                for c in range(CH):
                    pool.indirect_dma_start(out=gath[:, e % GBUF, c, :], out_offset=None, in_=h_rows[:, :],
                                            in_offset=bass.IndirectOffsetOnAxis(ap=rows[:, g, c, k:k + 1], axis=0),
                                            ).then_inc(s_gath[e % GBUF], 16)

            def scatter(e):
                g, k = divmod(e, 8)
                if e == 0:
                    pool.wait_ge(s_store, 16 * (NT // 4))
                else:
                    pool.wait_ge(s_scat, 16 * CH * e)
                for c in range(CH):
                    pool.wait_ge(s_eo, CH * e + c + 1)
                    pool.indirect_dma_start(out=out_rows, in_=eo[:, e % 2, c, :], in_offset=None,
                                            out_offset=bass.IndirectOffsetOnAxis(ap=rows[:, g, c, k:k + 1], axis=0),
                                            compute_op=ALU.add).then_inc(s_scat, 16)

            pool.wait_ge(s_hstore, 16 * NB)
            for e in range(GBUF - 1):
                gather(e)
                if e == 3:
                    shared_add(LAST)
            for e in range(E):
                if e + GBUF - 1 < E:
                    gather(e + GBUF - 1)
                scatter(e)

        def weigh(act, e):
            act.wait_ge(s_eb, e + 1)
            for c in range(CH):
                act.activation(eo[:, e % 2, c, :], eo[:, e % 2, c, :], ACT.Copy,
                               scale=gath[:, e % GBUF, c, C + e:C + e + 1]).then_inc(s_eo, 1)

        @block.scalar
        def _(act):
            def diagonals(first, scales):
                for k, scale in enumerate(scales):
                    last = act.activation(diag[:, first + k, :], ident[:, :], ACT.Copy, scale=scale)
                last.then_inc(s_diag, 1)

            def norm_tiles(those, dst, src):
                for i in those:
                    last = act.activation(dst(i), src(i), ACT.Identity, bias=shift[:, i:i + 1],
                                          scale=rstd[:, i:i + 1])
                return last

            def norm_x(b):
                act.wait_ge(s_shift, b + 1)
                norm_tiles(range(8 * b + 1, 8 * b + 8, 2), lambda i: xn_tok[:, i, :],
                           lambda i: x_tok[:, i, :]).then_inc(s_xna, 1)

            def keep_xp(b, r):
                act.wait_ge(s_xnT, 2 * b + r + 1)
                act.copy(xp[:, r, b, 1:N1 + 1], bank[2 * b + r][:, :]).then_inc(s_xp, 1)

            act.wait_ge(s_ident, 1)
            act.wait_ge(s_const, 16)
            diagonals(0, [taps[:, 4 + k:5 + k] for k in range(4)])
            norm_x(0)
            act.wait_ge(s_pad, 1)
            keep_xp(0, 0)
            keep_xp(0, 1)
            norm_x(1)
            keep_xp(1, 0)
            keep_xp(1, 1)
            act.wait_ge(s_comb, 1)
            diagonals(9, [tap_sum(1, k) for k in range(5)])
            diagonals(4, [tap_sum(0, k) for k in range(5)])
            act.wait_ge(s_h1, 1)
            act.copy(h1p[:, 0, 1:N1 + 1], bank[4][:, :]).then_inc(s_h1a, 1)
            act.wait_ge(s_l2, 1)
            act.activation(expf[:, :], l2f[:, :], ACT.Exp).then_inc(s_exp, 1)
            act.wait_ge(s_qvT, 1)
            act.copy(vT[:, :], bank[6][:, :]).then_inc(s_vT, 1)
            act.wait_ge(s_qvT, 2)
            act.copy(kT[:, :], bank[7][:, :]).then_inc(s_kT, 1)
            act.wait_ge(s_attnT, 2)
            act.copy(ap_[:, 1, 1:N2 + 1], bank[7][:, 0:N2]).then_inc(s_apa, 1)
            for b in range(NB):
                act.wait_ge(s_up2, b + 1)
                act.copy(r1p[:, b, 2:N1 + 2:2], bank[5 + b][:, 0:N2]).then_inc(s_r1a, 1)

            def normalise_sum(g):
                act.wait_ge(s_shift, norm_no("t", g))
                norm_tiles(range(4 * g, 4 * g + 4), lambda i: x1[:, i, :], psum_t).then_inc(s_aff, 1)

            def features(g):
                act.wait_ge(s_shift, norm_no("x1", g))
                norm_tiles(range(4 * g, 4 * g + (2 if g == LAST else 4)), lambda i: hrow[:, i, 0:C],
                           lambda i: x1[:, i, :]).then_inc(s_hna, 1)

            def keep_hT(g):
                act.wait_ge(s_hTp, g + 1)
                act.copy(hT[:, group(g), :].rearrange("p i t -> p (i t)"), bank[6 + g % 2][:, :]).then_inc(s_hT, 1)

            normalise_sum(0)
            normalise_sum(1)
            for g in range(LAST + 1):
                if g + 2 <= LAST:
                    normalise_sum(g + 2)
                features(g)
                if g:
                    keep_hT(g - 1)
            keep_hT(LAST)
            act.wait_ge(s_logit, 1)
            act.activation(sel[:, 0, :], bank[4][:, 0:256], ACT.Sigmoid).then_inc(s_score, 1)
            act.wait_ge(s_score, 1)
            act.copy(hrow[:, :, C:ROW].rearrange("p (k r) e -> p k r e", r=2),
                     sel[:, 0, :].rearrange("p (r e k) -> p k r e", r=2, e=E)).then_inc(s_hrow, 1)
            def keep_down(n):
                act.wait_ge(s_shout, n + 1)
                if n:
                    act.wait_ge(s_base, n)
                act.copy(sh_down[:, :], bank[4][:, :]).then_inc(s_shdn, 1)

            for n in range(LAST + 1):
                for t in range(SHT):
                    if n:
                        act.wait_ge(s_shhid, SHT * (n - 1) + t + 1)
                    act.wait_ge(s_shg, SHT * n + t + 1)
                    act.activation(sgate[:, t, :], bank[t][:, :], ACT.Silu).then_inc(s_shsil, 1)
                    act.wait_ge(s_shu, SHT * n + t + 1)
                    act.copy(sh_up[:, t, :], bank[2 + t][:, :]).then_inc(s_shupe, 1)
                if n:
                    keep_down(n - 1)
            keep_down(LAST)
            for q in range(E * FT):
                e, j = divmod(q, FT)
                act.wait_ge(s_gu, q + 1)
                if q >= SGB:
                    act.wait_ge(s_hid, q - SGB + 1)
                act.activation(sgate_e[:, q % SGB, :], up_bank(q)[:, CAP:2 * CAP], ACT.Silu,
                               bias=biasT[:, 1, j, e:e + 1]).then_inc(s_sil, 1)
                if j == 2 and e > 0:
                    weigh(act, e - 1)
            weigh(act, E - 1)

        @block.vector
        def _(dve):
            step = [0]

            def link(ins):
                step[0] += 1
                ins.then_inc(s_dve, 1)
                dve.wait_ge(s_dve, step[0])

            def row_stats(n, src):
                w = norm_tiles_of(n)
                for i in range(w.start, w.stop):
                    last = dve.bn_stats(stats[:, i, :], src(i))
                link(last)
                for i in range(w.start, w.stop):
                    last = dve.bn_aggr(mean_var[:, i, :], stats[:, i, :])
                link(last)
                dve.tensor_scalar(var_eps[:, w], mean_var[:, w, 1], LN_EPS, None, ALU.add).then_inc(s_stats, 1)

            def norm_shift(n):
                w = norm_tiles_of(n)
                dve.wait_ge(s_rstd, n)
                dve.scalar_tensor_tensor(shift[:, w], mean_var[:, w, 0], -1.0, rstd[:, w], ALU.mult, ALU.mult).then_inc(s_shift, 1)

            def norm_tiles(those, dst, src):
                for i in those:
                    last = dve.tensor_scalar(dst(i), src(i), rstd[:, i:i + 1], shift[:, i:i + 1], ALU.mult, ALU.add)
                return last

            dve.wait_ge(s_ident, 1)
            dve.tensor_reduce(pick[:, :], ident[:, :].rearrange("p (a e) -> p e a", e=8), AX.X, ALU.add)
            tok = lambda i: x_tok[:, i, :]
            dve.wait_ge(s_x[0], 16)
            row_stats(1, tok)
            dve.wait_ge(s_const, 16)
            syn = taps[:, 8:16].rearrange("p (f k) -> p f k", f=2)
            dve.tensor_tensor(comb[:, :, 0:1], syn[:, :, 0:1], syn[:, :, 1:2], ALU.add)
            dve.tensor_tensor(comb[:, :, 1:2], syn[:, :, 2:3], syn[:, :, 3:4], ALU.add)
            dve.tensor_tensor(comb[:, :, 2:3], syn[:, :, 1:2], syn[:, :, 2:3], ALU.add).then_inc(s_comb, 1)
            dve.wait_ge(s_x[1], 16)
            row_stats(2, tok)
            for b in range(NB):
                norm_shift(b + 1)
                dve.wait_ge(s_shift, b + 1)
                norm_tiles(range(8 * b, 8 * b + 8, 2), lambda i: xn_tok[:, i, :], tok).then_inc(s_xnv, 1)
            for b in range(NB):
                dve.wait_ge(s_xp, 2 * b + 2)
                dst = l1p[:, b, 1:N1 + 1]
                for k, (r, o) in enumerate(PHASE):
                    src = xp[:, r, b, o:o + N1]
                    if k == 0:
                        ins = dve.tensor_scalar(dst, src, taps[:, 0:1], None, ALU.mult)
                    else:
                        ins = dve.scalar_tensor_tensor(dst, src, taps[:, k:k + 1], dst, ALU.mult, ALU.add)
                    if k < 3:
                        link(ins)
                ins.then_inc(s_l1, 1)
            dve.wait_ge(s_l1, NB)

            def level2(dst, t0):
                link(dve.tensor_scalar(dst, l1p[:, :, 0:N1:2], taps[:, t0:t0 + 1], None, ALU.mult))
                for k in range(1, 4):
                    ins = dve.scalar_tensor_tensor(dst, l1p[:, :, k:k + N1:2], taps[:, t0 + k:t0 + k + 1], dst,
                                                   ALU.mult, ALU.add)
                    if k < 3:
                        link(ins)
                return ins

            level2(l2f[:, :].rearrange("p (b n) -> p b n", b=NB), 0).then_inc(s_l2, 1)
            dve.wait_ge(s_l2, 1)
            link(dve.tensor_scalar(qf[:, :], l2f[:, :], 0.0, None, ALU.max))
            dve.wait_ge(s_exp, 1)
            dve.scalar_tensor_tensor(qf[:, :], expf[:, :], 1.0, qf[:, :], ALU.min, ALU.add).then_inc(s_q, 1)
            dve.wait_ge(s_q, 1)
            link(dve.tensor_reduce(zsum[:, :], qf[:, :].rearrange("p (b n) -> p b n", b=NB), AX.X, ALU.add))
            dve.wait_ge(s_masks, 1)
            for b in range(NB):
                dve.tensor_scalar(kvz[:, b, C:], same8[:, 0:P:HEAD], zsum[:, b:b + 1], None, ALU.mult)
            level2(h2p[:, :, 1:N2 + 1], 4).then_inc(s_h2, 1)
            dve.wait_ge(s_kv, 1)
            dve.tensor_tensor(kvz[:, :, 0:C], bank[6][:, 0:256].rearrange("p (b n) -> p b n", b=NB),
                              same8[:, :].unsqueeze(1).to_broadcast([P, NB, P]), ALU.mult).then_inc(s_kvm, 1)
            dve.wait_ge(s_nd, 1)
            nd = [bank[6 + b][:, 0:2 * (C + 16)].rearrange("p (t c) -> p t c", t=2) for b in range(NB)]
            dve.tensor_scalar(rden[:, 0, :, :], nd[0][:, :, C:], ATTN_EPS, None, ALU.add)
            link(dve.tensor_scalar(rden[:, 1, :, :], nd[1][:, :, C:], ATTN_EPS, None, ALU.add))
            link(dve.reciprocal(rden[:, :, :, :], rden[:, :, :, :]))
            for b in range(NB):
                dve.tensor_tensor(attn_tok[:, b, :, :].rearrange("p t (h d) -> p t h d", d=HEAD),
                                  nd[b][:, :, 0:C].rearrange("p t (h d) -> p t h d", d=HEAD),
                                  rden[:, b, :, :].unsqueeze(3).to_broadcast([P, N2 // P, C // HEAD, HEAD]),
                                  ALU.mult).then_inc(s_attn, 1)
            dve.wait_ge(s_attnT, 1)
            dve.tensor_copy(ap_[:, 0, 1:N2 + 1], bank[6][:, 0:N2]).then_inc(s_apv, 1)
            dve.wait_ge(s_up2h, 1)
            for b in range(NB):
                dve.wait_ge((s_apv, s_apa)[b], 1)
                dst = r1p[:, b, 1:N1 + 1:2]
                for k, o in TAPS[0]:
                    ins = dve.scalar_tensor_tensor(dst, ap_[:, b, o:o + N2], tap_sum(0, k),
                                                   dst if k else bank[4][:, b * N2:(b + 1) * N2], ALU.mult, ALU.add)
                    if k < 2:
                        link(ins)
                ins.then_inc(s_r1v, 1)

            def x1_t(i):
                return x1[:, i, :]

            def stats_of_sum(g):
                dve.wait_ge(s_up1, g + 1)
                row_stats(norm_no("t", g), psum_t)

            def block_out(g):
                dve.wait_ge(s_aff, g + 1)
                link(dve.tensor_tensor(x1[:, group(g), :], x1[:, group(g), :],
                                       gamma_bc.unsqueeze(1).to_broadcast([P, 4, C]), ALU.mult))
                if g == 0:
                    dve.wait_ge(s_xb, 1)
                dve.tensor_tensor(x1[:, group(g), :], x1[:, group(g), :], x_tok[:, group(g), :], ALU.add).then_inc(s_x1b, 1)

            def stats_of_x1(g):
                dve.wait_ge(s_x1b, g + 1)
                row_stats(norm_no("x1", g), x1_t)

            stats_of_sum(0)
            norm_shift(norm_no("t", 0))
            for g in range(LAST + 1):
                if g < LAST:
                    stats_of_sum(g + 1)
                block_out(g)
                if g:
                    norm_shift(norm_no("x1", g - 1))
                if g < LAST:
                    norm_shift(norm_no("t", g + 1))
                stats_of_x1(g)
            norm_shift(norm_no("x1", LAST))
            dve.wait_ge(s_shift, len(NORMS))
            norm_tiles(range(4 * LAST + 2, 4 * LAST + 4), lambda i: hrow[:, i, 0:C], x1_t).then_inc(s_hnv, 1)
            dve.wait_ge(s_scT, 1)
            link(dve.tensor_copy(score2[:, :].rearrange("p (t r) -> p r t", r=2),
                                 bank[5][:, 0:256].rearrange("p (r t) -> p r t", r=2)))
            high, low1, both = (key[:, k, :] for k in range(3))
            link(dve.tensor_scalar(bits[:, 0, :], score2[:, :].bitcast(I32), LOW, None, ALU.arith_shift_right))
            dve.tensor_copy(high, bits[:, 0, :])
            thr, reached, cand, base, ktab = (search[:, a:b] for a, b in ((0, 1), (1, 2), (2, 5), (5, 8), (8, 11)))
            dve.memset(thr, 0.0)
            for k in range(3):
                dve.memset(cand[:, k:k + 1], float((k + 1) << ROUNDS[0]))
                last = dve.memset(ktab[:, k:k + 1], float(k + 1))
            link(last)
            keys = high
            for r, bit in enumerate(ROUNDS):
                for k in range(3):
                    last = dve.tensor_scalar(junk[:, k, :], keys, cand[:, k:k + 1], 0.0, ALU.is_ge, ALU.add,
                                             accum_out=cnt[:, k:k + 1])
                last.then_inc(s_cnt, 1)
                if r == 0:
                    link(dve.tensor_scalar(bits[:, 1, :], score2[:, :].bitcast(I32), (1 << LOW) - 1, None, ALU.bitwise_and))
                    dve.tensor_scalar(low1, bits[:, 1, :], 1.0, None, ALU.add)
                if bit:
                    dve.wait_ge(s_dve, step[0])
                    link(dve.scalar_tensor_tensor(base, ktab, float(1 << (bit - 2)), thr.to_broadcast([P, 3]), ALU.mult, ALU.add))
                dve.wait_ge(s_tot, r + 1)
                link(dve.tensor_scalar(search[:, 11:14], bank[5][:, 509:512], float(CAP), 0.0, ALU.is_ge, ALU.add,
                                       accum_out=reached))
                if bit:
                    link(dve.scalar_tensor_tensor(cand, reached.to_broadcast([P, 3]), float(1 << bit), base, ALU.mult, ALU.add))
                ins = dve.scalar_tensor_tensor(thr, reached, float(1 << bit), thr, ALU.mult, ALU.add)
                step[0] += 1
                ins.then_inc(s_dve, 1)
                if not bit:
                    dve.wait_ge(s_dve, step[0])
                    if keys is high:
                        dve.tensor_scalar(junk[:, 0, :], high, thr, float(1 << (LOW + 1)), ALU.is_gt, ALU.mult)
                        link(dve.scalar_tensor_tensor(both, high, thr, low1, ALU.is_equal, ALU.mult))
                        dve.tensor_tensor(both, both, junk[:, 0, :], ALU.max)
                        dve.memset(thr, 1.0)
                        for k in range(3):
                            last = dve.memset(cand[:, k:k + 1], float(((k + 1) << ROUNDS[r + 1]) + 1))
                        link(last)
                        keys = both

            gt, eq, scan_gt, scan_eq, slot_eq = (sel[:, k, :] for k in range(5))
            slot_gt = score2[:, :]
            dve.tensor_scalar(gt, both, thr, 0.0, ALU.is_gt, ALU.add, accum_out=cnt[:, 1:2])
            dve.tensor_scalar(eq, both, thr, 0.0, ALU.is_equal, ALU.add,
                              accum_out=cnt[:, 2:3]).then_inc(s_cnt, 1)
            dve.wait_ge(s_cnt, len(ROUNDS) + 1)
            dve.tensor_tensor_scan(scan_gt, gt, gt, 0.0, ALU.add, ALU.max)
            link(dve.tensor_tensor_scan(scan_eq, eq, eq, 0.0, ALU.add, ALU.max))
            dve.wait_ge(s_tot, len(ROUNDS) + 1)
            dve.scalar_tensor_tensor(slot_gt, scan_gt, bank[5][:, 510:511], gt, ALU.add, ALU.mult)
            dve.scalar_tensor_tensor(slot_eq, scan_eq, bank[5][:, 511:512], eq, ALU.add, ALU.mult).then_inc(s_pos, 1)
            dve.wait_ge(s_posT, 1)
            link(dve.tensor_scalar(slot_i[:, 0, :].rearrange("p (r k e) -> p r k e", r=2, k=BLK),
                                   bank[5][:, 0:256].rearrange("p (r e k) -> p r k e", r=2, k=BLK),
                                   -1.0, None, ALU.add))
            dve.tensor_scalar(slot_i[:, 1, :], slot_i[:, 0, :], 4, None, ALU.arith_shift_right)
            link(dve.tensor_scalar(slot_i[:, 2, :], slot_i[:, 0, :], HI - 1, None, ALU.bitwise_and))
            link(dve.tensor_copy(slot_h[:, :, :], slot_i[:, 1:3, :]))

            def one_hot(dst, k, g):
                part = slot_h[:, k, :].rearrange("p (n e) -> p n e", e=8)[:, g::2, :]
                for a in range(HI):
                    last = dve.tensor_scalar(dst[:, g::2, a, :], part, float(a), None, ALU.is_equal)
                return last

            def times_token(g):
                lo = one_lo[:, g::2, :, :]
                tok_g = token_no[:, :].rearrange("p (n e) -> p n e", e=8)[:, g::2, :]
                return dve.tensor_tensor(lo, lo, tok_g.unsqueeze(2).to_broadcast([P, NT, HI, 8]), ALU.mult)

            def own_expert(g):
                dve.wait_ge(s_tab, g + 1)
                link(dve.tensor_tensor(ext[:, 0:P].rearrange("p (b e) -> p b e", e=8),
                                       bank[6 + g][:, 0:P].rearrange("p (b e) -> p b e", e=8),
                                       pick[:, :].unsqueeze(1).to_broadcast([P, HI, 8]), ALU.mult))
                dve.tensor_reduce(itab[:, g * HI:(g + 1) * HI], ext[:, 0:P].rearrange("p (b e) -> p b e", e=8), AX.X,
                                  ALU.add).then_inc(s_itab, 1)

            def keep_table(g):
                dve.wait_ge(s_itT, g + 1)
                dve.tensor_copy(itabT[:, g * P:(g + 1) * P], bank[5][0:HI, 0:P]).then_inc(s_itTe, 1)

            def slot_rows(g):
                dve.wait_ge(s_spread, g + 1)
                link(dve.tensor_tensor(ext[:, P:2 * P].rearrange("p (g e a) -> p g e a", g=CH, e=8),
                                       bank[5][:, P:2 * P].rearrange("p (g a e) -> p g e a", g=CH, e=8),
                                       pick[:, :].unsqueeze(1).unsqueeze(1).to_broadcast([P, CH, 8, 8]), ALU.mult))
                dve.tensor_reduce(rows[:, g, :, :].rearrange("p c e -> p (c e)"),
                                  ext[:, P:2 * P].rearrange("p (m a) -> p m a", a=8), AX.X, ALU.add).then_inc(s_rows, 1)

            link(one_hot(one_lo, 1, 0))
            times_token(0)
            one_hot(one_hi, 0, 0).then_inc(s_hot, 1)
            link(one_hot(one_lo, 1, 1))
            own_expert(0)
            times_token(1)
            keep_table(0)
            one_hot(one_hi, 0, 1).then_inc(s_hot, 1)
            slot_rows(0)
            own_expert(1)
            keep_table(1)
            slot_rows(1)

            def keep_x(e):
                dve.wait_ge(s_xsT, e + 1)
                if e >= 2:
                    dve.wait_ge(s_gu, FT * (e - 1))
                dve.tensor_copy(xselT[:, e % 2, :], bank[5][:, 0:CAP]).then_inc(s_xs, 1)

            def add_bias(e):
                dve.wait_ge(s_dn, e + 1)
                if e >= 2:
                    dve.wait_ge(s_scat, 16 * CH * (e - 1))
                dve.tensor_tensor(eo[:, e % 2, :, :], bank[3 + e % 2][:, 0:CAP].rearrange("p (c d) -> p c d", c=CH),
                                  down_b_bc[:, e, :].unsqueeze(1).to_broadcast([P, CH, C]), ALU.add).then_inc(s_eb, 1)

            dve.wait_ge(s_db_in, 16)
            keep_x(0)
            for q in range(E * FT):
                e, j = divmod(q, FT)
                dve.wait_ge(s_sil, q + 1)
                if e >= 2:
                    dve.wait_ge(s_dn, e - 1)
                dve.scalar_tensor_tensor(hidden[:, e % 2, j, :], up_bank(q)[:, 0:CAP], biasT[:, 0, j, e:e + 1],
                                         sgate_e[:, q % SGB, :], ALU.add, ALU.mult).then_inc(s_hid, 1)
                if j == 1 and e > 0:
                    add_bias(e - 1)
                if j == 2 and e + 1 < E:
                    keep_x(e + 1)
            add_bias(E - 1)

        @block.tensor
        def _(pe):
            pe.wait_ge(s_ident, 1)
            def stay_warm(n, spare):
                for _ in range(n):
                    pe.matmul(spare[:, 0:P], ident[:, :], ident[:, :], start=True, stop=True)

            stay_warm(18, bank[7])
            for b in range(NB):
                for r in range(2):
                    pe.wait_ge((s_xnv, s_xna)[r], b + 1)
                    for k in range(BPB):
                        last = pe.transpose(bank[2 * b + r][:, k * P:(k + 1) * P], xn_tok[:, 2 * (b * BPB + k) + r, :],
                                            ident[:, :])
                    last.then_inc(s_xnT, 1)
            pe.wait_ge(s_diag, 1)
            pe.wait_ge(s_xp, 2)
            for k, (r, o) in enumerate(PHASE):
                last = pe.matmul(bank[4][:, :], diag[:, k, :], xp[:, r, 0, o:o + N1], start=(k == 0), stop=(k == 3))
            last.then_inc(s_h1, 1)

            def place(n, t):
                blk, par = divmod(4 * n + t, 2)
                return blk // BPB, par, (blk % BPB) * P, bank[n][:, t * P:(t + 1) * P]

            def add_xn(n):
                pe.wait_ge(s_xp, 2 * (n // 2) + 2)
                for t in range(4):
                    b, par, m0, dst = place(n, t)
                    pe.matmul(dst, xp[:, par, b, m0 + 1:m0 + 1 + P], ident[:, :], start=(t == 0), stop=False,
                              skip_group_check=True)

            def synth(n, those, band, d0):
                for t in those:
                    b, par, m0, dst = place(n, t)
                    for k, o in TAPS[par]:
                        last = pe.matmul(dst, band[:, b, m0 + o:m0 + o + P], diag[:, d0 + k, :], start=False,
                                         stop=(d0 == 4 and o == 2), skip_group_check=True)
                return last

            def synth2_high(n, those=range(4)):
                if n // 2 == 0:
                    pe.wait_ge(s_h1a, 1)
                else:
                    pe.wait_ge(s_h1p, 1)
                pe.wait_ge(s_diag, 2)
                synth(n, those, h1p, 9)

            def synth2_low(n):
                pe.wait_ge(s_diag, 3)
                pe.wait_ge(s_r1v, n // 2 + 1)
                pe.wait_ge(s_r1a, n // 2 + 1)
                synth(n, range(4), r1p, 4).then_inc(s_up1, 1)

            add_xn(0)
            add_xn(1)
            synth2_high(0)
            pe.wait_ge(s_l2, 1)
            for k in range(4):
                last = pe.transpose(bank[6][:, k * P:(k + 1) * P], l2f[:, k * P:(k + 1) * P], ident[:, :])
            last.then_inc(s_qvT, 1)
            add_xn(2)
            pe.wait_ge(s_q, 1)
            for k in range(4):
                last = pe.transpose(bank[7][:, k * P:(k + 1) * P], qf[:, k * P:(k + 1) * P], ident[:, :])
            last.then_inc(s_qvT, 1)
            add_xn(3)
            pe.wait_ge(s_vT, 1)
            pe.wait_ge(s_kT, 1)
            for b in range(NB):
                for k in range(2):
                    o = (2 * b + k) * P
                    last = pe.matmul(bank[6][:, b * P:(b + 1) * P], kT[:, o:o + P], vT[:, o:o + P],
                                     start=(k == 0), stop=(k == 1))
            last.then_inc(s_kv, 1)
            synth2_high(1, (0, 1))
            pe.wait_ge(s_kvm, 1)
            for b in range(NB):
                for t in range(2):
                    o = (2 * b + t) * P
                    last = pe.matmul(bank[6 + b][:, t * (C + 16):(t + 1) * (C + 16)], qf[:, o:o + P], kvz[:, b, :],
                                     start=True, stop=True)
            last.then_inc(s_nd, 1)
            pe.wait_ge(s_h2, 1)
            for k, o in TAPS[0]:
                last = pe.matmul(bank[4][:, :], diag[:, 9 + k, :], h2p[:, :, o:o + N2], start=(k == 0), stop=(o == 2))
            last.then_inc(s_up2h, 1)
            for b in range(NB):
                pe.wait_ge(s_attn, b + 1)
                for t in range(2):
                    last = pe.transpose(bank[6 + b][:, t * P:(t + 1) * P], attn_tok[:, b, t, :], ident[:, :])
                last.then_inc(s_attnT, 1)
            def synth1_odd(b, band, d0):
                for k, o in TAPS[1]:
                    last = pe.matmul(bank[5 + b][:, 0:N2], diag[:, d0 + k, :], band[:, b, o:o + N2],
                                     start=(d0 == 9 and k == 3), stop=(d0 == 4 and o == 2), skip_group_check=True)
                return last

            synth1_odd(0, h2p, 9)
            pe.wait_ge(s_diag, 3)
            pe.wait_ge(s_apv, 1)
            synth1_odd(0, ap_, 4).then_inc(s_up2, 1)
            synth1_odd(1, h2p, 9)
            synth2_low(0)
            pe.wait_ge(s_apa, 1)
            synth1_odd(1, ap_, 4).then_inc(s_up2, 1)
            synth2_high(1, (2, 3))
            synth2_low(1)
            for n in (2, 3):
                synth2_high(n)
                synth2_low(n)

            def features_T(n):
                pe.wait_ge(s_hna, n + 1)
                if n == LAST:
                    pe.wait_ge(s_hnv, 1)
                if n >= 2:
                    pe.wait_ge(s_hT, n - 1)
                for t in range(4):
                    last = pe.transpose(bank[6 + n % 2][:, t * P:(t + 1) * P], hrow[:, 4 * n + t, 0:C], ident[:, :])
                last.then_inc(s_hTp, 1)

            def router(n):
                pe.wait_ge(s_hT, n + 1)
                for i in range(4 * n, 4 * n + 4):
                    blk, par = divmod(i, 2)
                    o = par * P + blk
                    last = pe.matmul(bank[4][:, o:par * P + P:BLK], hT[:, i, :], gate_wT, start=True, stop=True)
                return last

            BEFORE_HT, BEFORE_TABLE, BEFORE_SCORES, BEFORE_SEARCH, IN_ROUND = (8, 8, 2, 4), 2, 3, 3, 3
            for g in range(LAST + 1):
                pe.wait_ge(s_x1b, g + 1)
                stay_warm(BEFORE_HT[g], bank[5])
                features_T(g)
                if g:
                    router(g - 1)
            last = router(LAST)
            last.then_inc(s_logit, 1)
            stay_warm(BEFORE_SCORES, bank[6])
            pe.wait_ge(s_score, 1)
            for r in range(2):
                last = pe.transpose(bank[5][:, r * P:(r + 1) * P], sel[:, 0, r * P:(r + 1) * P], ident[:, :])
            last.then_inc(s_scT, 1)
            pe.wait_ge(s_masks, 1)

            def count(n):
                pe.wait_ge(s_cnt, n)
                pe.matmul(bank[5][:, 509:512], same8_bf[:, :], cnt[:, 0:3], start=True, stop=True).then_inc(s_tot, 1)

            def shared_up(n, t, kind):
                if n:
                    pe.wait_ge((s_shsil, s_shupe)[kind], SHT * (n - 1) + t + 1)
                rhs = hT[:, 4 * n:4 * n + 4, :].rearrange("p i t -> p (i t)")
                pe.matmul(bank[2 * kind + t][:, :], sh_wT[:, 2 * kind + t, :], rhs, start=True,
                          stop=True).then_inc((s_shg, s_shu)[kind], 1)

            def shared_down(n, t):
                pe.wait_ge(s_shhid, SHT * (n + 1))
                if n:
                    pe.wait_ge(s_shdn, n)
                for k in range(SHT):
                    last = pe.matmul(bank[4][:, t * P:(t + 1) * P], sh_hid[:, n % 2, k, t * P:(t + 1) * P], sh_wT[:, 4 + k, :],
                                     start=(k == 0), stop=(k == SHT - 1))
                if t == 3:
                    last.then_inc(s_shout, 1)

            stay_warm(BEFORE_SEARCH, bank[6])
            pe.wait_ge(s_shw, 16)
            pe.wait_ge(s_scT, 1)
            for r in range(len(ROUNDS)):
                count(r + 1)
                n, part = divmod(r, PERIOD)
                if n < LAST and part < 4:
                    shared_up(n, part // 2, part % 2)
                    if n:
                        shared_down(n - 1, part)
                else:
                    stay_warm(IN_ROUND, bank[6])
            pe.wait_ge(s_cnt, len(ROUNDS) + 1)
            pe.matmul(bank[5][:, 510:511], earlier[:, :], cnt[:, 1:2], start=True, stop=True)
            pe.matmul(bank[5][:, 511:512], same8_bf[:, :], cnt[:, 1:2], start=True, stop=False)
            pe.matmul(bank[5][:, 511:512], earlier[:, :], cnt[:, 2:3], start=False, stop=True).then_inc(s_tot, 1)
            pe.wait_ge(s_pos, 1)
            for r in range(2):
                pe.matmul(bank[5][:, r * P:(r + 1) * P], score2[:, r:256:2], ident[:, :], start=True, stop=False)
                last = pe.matmul(bank[5][:, r * P:(r + 1) * P], sel[:, 4, r:256:2], ident[:, :], start=False, stop=True)
            last.then_inc(s_posT, 1)
            for t in range(4):
                shared_down(LAST - 1, t)
                shared_up(LAST, t // 2, t % 2)

            def table(g):
                pe.wait_ge(s_hot, g + 1)
                for i in range(NT):
                    n = 2 * i + g
                    last = pe.matmul(bank[6 + g][:, 0:P], one_hi[:, n, :, :].rearrange("p a e -> p (a e)"),
                                     one_lo[:, n, :, :].rearrange("p b e -> p (b e)"), start=(i == 0), stop=(i == NT - 1))
                last.then_inc(s_tab, 1)

            def turn_table(g):
                pe.wait_ge(s_itab, g + 1)
                pe.transpose(bank[5][0:HI, 0:P], itab[:, g * HI:(g + 1) * HI], ident[:, :]).then_inc(s_itT, 1)

            def spread(g):
                pe.wait_ge(s_itTe, g + 1)
                pe.matmul(bank[5][:, P:2 * P], sel_lo[:, :], itabT[:, g * P:(g + 1) * P], start=True,
                          stop=True).then_inc(s_spread, 1)

            table(0)
            turn_table(0)
            spread(0)
            table(1)
            pe.wait_ge(s_shupe, SHT * (LAST + 1))
            stay_warm(BEFORE_TABLE, bank[3])
            pe.wait_ge(s_rows, 1)
            turn_table(1)
            spread(1)

            def turn_x(e):
                pe.wait_ge(s_gath[e % GBUF], 16 * CH * (e // GBUF + 1))
                if e == 0:
                    pe.wait_ge(s_rows, 2)
                else:
                    pe.wait_ge(s_xs, e)
                for c in range(CH):
                    last = pe.transpose(bank[5][:, c * P:(c + 1) * P], gath[:, e % GBUF, c, 0:C], ident[:, :])
                last.then_inc(s_xsT, 1)

            LAG = 3

            def down(q):
                e, j = divmod(q, FT)
                pe.wait_ge(s_hid, q + 1)
                if q == FT:
                    pe.wait_ge(s_base, NT // 4)
                if j == 0 and e >= 2:
                    pe.wait_ge(s_eb, e - 1)
                for c in range(CH):
                    last = pe.matmul(bank[3 + e % 2][:, c * P:(c + 1) * P], hidden[:, e % 2, j, c * P:(c + 1) * P],
                                     wT[:, e, 2, j, :], start=(j == 0 and c == 0), stop=(j == FT - 1),
                                     skip_group_check=True)
                if j == FT - 1:
                    last.then_inc(s_dn, 1)

            for t in range(4):
                shared_down(LAST, t)
            turn_x(0)
            for q in range(E * FT):
                e, j = divmod(q, FT)
                if j == 0:
                    pe.wait_ge(s_wT[e], 16)
                    pe.wait_ge(s_xs, e + 1)
                if q >= len(UP_BANKS):
                    pe.wait_ge(s_hid, q - len(UP_BANKS) + 1)
                pe.matmul(up_bank(q)[:, 0:CAP], wT[:, e, 0, j, :], xselT[:, e % 2, :], start=True, stop=True)
                pe.matmul(up_bank(q)[:, CAP:2 * CAP], wT[:, e, 1, j, :], xselT[:, e % 2, :], start=True,
                          stop=True).then_inc(s_gu, 1)
                if q >= LAG:
                    down(q - LAG)
                if j == 1 and e + 1 < E:
                    turn_x(e + 1)
            for q in range(E * FT - LAG, E * FT):
                down(q)


_OUTS = [((2, 1024, 128), 'float32')]


def _laid_out(inputs):
    import numpy as np
    v = {k: np.asarray(a) for k, a in inputs.items()}
    attn = lambda n: v["L0_attn_" + n]
    ffn = lambda n: v["L0_ffn_" + n]
    E, F, D = ffn("up_w").shape
    ft, sh = F // 128, ffn("sh_up_w").shape[0] // 128
    bias = [b.reshape(E, ft, 128).transpose(2, 1, 0).reshape(128, ft * E) for b in (ffn("up_b"), ffn("gb"))]
    packed = np.concatenate([attn(n).T for n in ("h_filter", "g_filter", "h_synth", "g_synth")]
                            + [ffn("gate_w").T] + bias
                            + [np.broadcast_to(attn(n), (128, D)) for n in ("norm_gamma", "norm_beta")], axis=1)
    rise = [w.reshape(E, ft, 128, D).transpose(0, 3, 1, 2) for w in (ffn("up_w"), ffn("gw"))]
    fall = ffn("down_w").reshape(E, D, ft, 128).transpose(0, 3, 2, 1)
    weights = np.stack(rise + [fall], axis=2)
    s_rise = [w.reshape(sh, 128, D).transpose(2, 0, 1) for w in (ffn("sh_gate_w"), ffn("sh_up_w"))]
    s_fall = ffn("sh_down_w").reshape(D, sh, 128).transpose(2, 1, 0)
    shared = np.concatenate(s_rise + [s_fall], axis=1)
    return {n: np.ascontiguousarray(a) for n, a in (("x", attn("x")), ("packed", packed), ("weights", weights),
                                                    ("shared", shared), ("down_b", ffn("down_b")))}


def kernel(**inputs):
    import numpy as _np
    import concourse.bacc as _bacc
    from concourse import mybir as _mybir
    from concourse.bass_utils import run_bass_kernel_spmd as _run

    nc = _bacc.Bacc("TRN2", target_bir_lowering=False, num_devices=1)
    arrays, args = {}, []
    for name, a in _laid_out(inputs).items():
        arrays[f"in_{name}_dram"] = a
        args.append(nc.dram_tensor(f"in_{name}_dram", a.shape, _mybir.dt.from_np(a.dtype), kind="ExternalInput").ap())
    for i, (shape, dtype) in enumerate(_OUTS):
        dt = _mybir.dt.from_np(_np.dtype(dtype))
        args.append(nc.dram_tensor(f"out_{i}_dram", shape, dt, kind="ExternalOutput").ap())
    wavelet_attention_moe(nc, *args)
    r = _run(nc, [arrays], core_ids=[0])
    return r.results[0]["out_0_dram"]
```
